# Optimizing a Trainium2 kernel written in Bass

```python
import numpy as np
import jax
import jax.numpy as jnp

def _softmax(x, axis=-1):
    return jax.nn.softmax(x, axis=axis)

def _gelu(x):
    return jax.nn.gelu(x, approximate=True)

def _silu(x):
    return jax.nn.silu(x)

def _sigmoid(x):
    return jax.nn.sigmoid(x)

def _layernorm(x, axis=-1, eps=1e-05):
    m = jnp.mean(x, axis=axis, keepdims=True)
    v = jnp.var(x, axis=axis, keepdims=True)
    return (x - m) / jnp.sqrt(v + eps)

def _scatter_add(tgt, idx, src, axis=0):
    return tgt.at[idx].add(src)

def _segment_sum(src, seg, n):
    return jax.ops.segment_sum(src, seg, n)
kernel_name = 'mk_flamingo_gated_d1_seqx_r8_387c6b'

def setup_inputs(seed: int=0):
    np.random.seed(seed)
    _w = jnp.asarray

    def _rec_inputs():
        import jax
        import jax.numpy as jnp
        _rk = jax.random.key(seed)
        x = 0.5 + 0.2887 * jax.random.normal(jax.random.fold_in(_rk, 1), (4, 256, 256), jnp.float32)
        _lenS = 256 - jax.random.randint(jax.random.fold_in(_rk, 7), (4,), 0, max(1, 256 // 4) + 1, jnp.int32)
        _lenS2 = 256 - jax.random.randint(jax.random.fold_in(_rk, 8), (4,), 0, max(1, 256 // 4) + 1, jnp.int32)
        _ctx_512P = jax.random.normal(jax.random.fold_in(_rk, 11), (4, 16, 64), jnp.float32)
        _ctx_512c = jax.random.dirichlet(jax.random.fold_in(_rk, 511), 0.3 * jnp.ones((16,), jnp.float32), (4, 256))
        _ctx_512t = jnp.einsum('bsk,bkd->bsd', _ctx_512c, _ctx_512P)
        _ctx_512t = _ctx_512t * jax.lax.rsqrt(jnp.mean(jnp.square(_ctx_512t)) + 1e-12) * 0.953939
        ctx_512 = -0.000392918 + 0.999932 * (_ctx_512t + 0.3 * jax.random.normal(jax.random.fold_in(_rk, 611), (4, 256, 64), jnp.float32))
        _g = jax.random.normal(jax.random.fold_in(_rk, 9001), (2, 1), jnp.float32)
        _g = jnp.sign(_g) * jnp.maximum(jnp.abs(_g), 1.0) + (_g == 0) * 1.0
        g_xattn = _g[0]
        g_ffn = _g[1]
        return (x, ctx_512, g_xattn, g_ffn)
    x, ctx_512, g_xattn, g_ffn = _rec_inputs()

    def _L0_xattn_setup():
        import jax, jax.numpy as jnp
        import numpy as np
        B, N, D = (16, 256, 64)
        H = 4
        TOP_K_RATIO = 0.3
        key = jax.random.key(seed)
        k1, k2, k3, k4 = jax.random.split(key, 4)
        h = jax.random.normal(k1, (B, N, D), dtype=jnp.float32)
        adj_raw = jax.random.uniform(k2, (B, N, N), dtype=jnp.float32)
        lim = 1.0 / np.sqrt(D)
        Wq = jax.random.uniform(k3, (D, D), minval=-lim, maxval=lim, dtype=jnp.float32)
        Wk = jax.random.uniform(k4, (D, D), minval=-lim, maxval=lim, dtype=jnp.float32)
        gamma_raw = jnp.float32(-0.85)
        return {'h': h, 'adj_raw': adj_raw, 'Wq': Wq, 'Wk': Wk, 'gamma_raw': gamma_raw}
    _L0_xattn_all = _L0_xattn_setup()
    _L0_xattn_in = {k: v for k, v in _L0_xattn_all.items() if k in ('Wq', 'Wk', 'gamma_raw')}
    del _L0_xattn_all

    def _L0_ffn_setup():
        import jax, jax.numpy as jnp
        import numpy as np
        E, K = (12, 3)
        B, S, H, I = (2, 256, 256, 640)

        def _forward(x, Wr, br, w1, b1, w2, b2, Wp1, bp1, Wp2, bp2):
            logits = jnp.einsum('bsh,he->bse', x, Wr) + br
            probs = jax.nn.softmax(logits, axis=-1)
            top_vals, top_idx = jax.lax.top_k(probs, K)
            ew = jax.nn.softmax(top_vals, axis=-1)
            out = jnp.zeros_like(x)
            for e in range(E):
                sel = top_idx == e
                mask = sel.any(axis=-1)
                cnt = sel.sum()
                w_e = jnp.sum(jnp.where(sel, ew, 0.0)) / jnp.maximum(cnt, 1).astype(ew.dtype)
                h = jax.nn.relu(jnp.einsum('bsh,hi->bsi', x, w1[e]) + b1[e])
                h = jnp.einsum('bsi,ih->bsh', h, w2[e]) + b2[e]
                out = out + mask[..., None].astype(x.dtype) * (w_e * h)
            pooled = out.mean(axis=1)
            phi = jax.nn.sigmoid(jax.nn.relu(pooled @ Wp1 + bp1) @ Wp2 + bp2)
            phi_mask = (phi > 0.7).astype(out.dtype)[:, :, None]
            return out * (1.0 - phi_mask * 0.8)
        key = jax.random.key(seed)
        ks = jax.random.split(key, 8)
        sH = np.float32(1.0 / np.sqrt(H))
        sI = np.float32(1.0 / np.sqrt(I))
        sH2 = np.float32(1.0 / np.sqrt(H // 2))
        return {'hidden_states': jax.random.normal(ks[0], (B, S, H), jnp.float32), 'Wr': jax.random.normal(ks[1], (H, E), jnp.float32) * sH, 'br': jnp.zeros((E,), jnp.float32), 'w1': jax.random.normal(ks[2], (E, H, I), jnp.float32) * sH, 'b1': jnp.zeros((E, I), jnp.float32), 'w2': jax.random.normal(ks[3], (E, I, H), jnp.float32) * sI, 'b2': jnp.zeros((E, H), jnp.float32), 'Wp1': jax.random.normal(ks[4], (H, H // 2), jnp.float32) * sH, 'bp1': jnp.zeros((H // 2,), jnp.float32), 'Wp2': jax.random.normal(ks[5], (H // 2, 1), jnp.float32) * sH2, 'bp2': jnp.zeros((1,), jnp.float32)}
    _L0_ffn_all = _L0_ffn_setup()
    _L0_ffn_in = {k: v for k, v in _L0_ffn_all.items() if k in ('Wr', 'br', 'w1', 'b1', 'w2', 'b2', 'Wp1', 'bp1', 'Wp2', 'bp2')}
    del _L0_ffn_all
    return {'x': x, 'ctx_512': ctx_512, 'g_xattn': g_xattn, 'g_ffn': g_ffn, 'L0_xattn_Wq': _L0_xattn_in['Wq'], 'L0_xattn_Wk': _L0_xattn_in['Wk'], 'L0_xattn_gamma_raw': _L0_xattn_in['gamma_raw'], 'L0_ffn_Wr': _L0_ffn_in['Wr'], 'L0_ffn_br': _L0_ffn_in['br'], 'L0_ffn_w1': _L0_ffn_in['w1'], 'L0_ffn_b1': _L0_ffn_in['b1'], 'L0_ffn_w2': _L0_ffn_in['w2'], 'L0_ffn_b2': _L0_ffn_in['b2'], 'L0_ffn_Wp1': _L0_ffn_in['Wp1'], 'L0_ffn_bp1': _L0_ffn_in['bp1'], 'L0_ffn_Wp2': _L0_ffn_in['Wp2'], 'L0_ffn_bp2': _L0_ffn_in['bp2']}

def reference(x, ctx_512, g_xattn, g_ffn, L0_xattn_Wq, L0_xattn_Wk, L0_xattn_gamma_raw, L0_ffn_Wr, L0_ffn_br, L0_ffn_w1, L0_ffn_b1, L0_ffn_w2, L0_ffn_b2, L0_ffn_Wp1, L0_ffn_bp1, L0_ffn_Wp2, L0_ffn_bp2):
    import jax
    import jax.numpy as jnp

    def _L0_xattn_ref(h, adj_raw, Wq, Wk, gamma_raw):
        import jax, jax.numpy as jnp
        import numpy as np
        B, N, D = (16, 256, 64)
        H = 4
        TOP_K_RATIO = 0.3
        b, n, dm = h.shape
        d = dm // H
        Q = (h @ Wq.T).reshape(b, n, H, d).transpose(0, 2, 1, 3)
        K = (h @ Wk.T).reshape(b, n, H, d).transpose(0, 2, 1, 3)
        sim = jnp.einsum('bhnd,bhmd->bnm', Q, K) / (jnp.sqrt(jnp.float32(d)) * H)
        k = max(1, int(n * TOP_K_RATIO))
        topk_vals = jax.lax.top_k(sim, k)[0]
        threshold = topk_vals[:, :, -1:]
        sparse_mask = (sim >= threshold).astype(sim.dtype)
        A_learned = jax.nn.sigmoid(sim) * sparse_mask
        A_learned = (A_learned + jnp.swapaxes(A_learned, -1, -2)) * 0.5
        gamma = jax.nn.sigmoid(gamma_raw)
        return (1.0 - gamma) * adj_raw + gamma * A_learned

    def _L0_ffn_ref(hidden_states, Wr, br, w1, b1, w2, b2, Wp1, bp1, Wp2, bp2):
        import jax, jax.numpy as jnp
        import numpy as np
        E, K = (12, 3)
        B, S, H, I = (2, 256, 256, 640)

        def _forward(x, Wr, br, w1, b1, w2, b2, Wp1, bp1, Wp2, bp2):
            logits = jnp.einsum('bsh,he->bse', x, Wr) + br
            probs = jax.nn.softmax(logits, axis=-1)
            top_vals, top_idx = jax.lax.top_k(probs, K)
            ew = jax.nn.softmax(top_vals, axis=-1)
            out = jnp.zeros_like(x)
            for e in range(E):
                sel = top_idx == e
                mask = sel.any(axis=-1)
                cnt = sel.sum()
                w_e = jnp.sum(jnp.where(sel, ew, 0.0)) / jnp.maximum(cnt, 1).astype(ew.dtype)
                h = jax.nn.relu(jnp.einsum('bsh,hi->bsi', x, w1[e]) + b1[e])
                h = jnp.einsum('bsi,ih->bsh', h, w2[e]) + b2[e]
                out = out + mask[..., None].astype(x.dtype) * (w_e * h)
            pooled = out.mean(axis=1)
            phi = jax.nn.sigmoid(jax.nn.relu(pooled @ Wp1 + bp1) @ Wp2 + bp2)
            phi_mask = (phi > 0.7).astype(out.dtype)[:, :, None]
            return out * (1.0 - phi_mask * 0.8)
        return _forward(hidden_states, Wr, br, w1, b1, w2, b2, Wp1, bp1, Wp2, bp2)
    x = x + jnp.tanh(g_xattn[0]) * _L0_xattn_ref(ctx_512, _layernorm(x, axis=-1), L0_xattn_Wq, L0_xattn_Wk, L0_xattn_gamma_raw)
    x = x + jnp.tanh(g_ffn[0]) * _L0_ffn_ref(_layernorm(x, axis=-1), L0_ffn_Wr, L0_ffn_br, L0_ffn_w1, L0_ffn_b1, L0_ffn_w2, L0_ffn_b2, L0_ffn_Wp1, L0_ffn_bp1, L0_ffn_Wp2, L0_ffn_bp2)
    return x

_drawn_inputs = setup_inputs


def setup_inputs(seed=0):
    import zlib

    import numpy as np

    out = dict(_drawn_inputs(seed))
    spreads = {'L0_ffn_br': (0.0, 0.1),
     'L0_ffn_b1': (0.0, 0.1),
     'L0_ffn_b2': (0.0, 0.1),
     'L0_ffn_bp1': (0.0, 0.1)}
    factors = {}
    for name, (base, spread) in spreads.items():
        noise = np.random.default_rng([zlib.crc32(name.encode()), seed]).standard_normal(out[name].shape)
        drawn = base * np.exp(spread * noise) if base else spread * noise
        out[name] = jnp.asarray(drawn.astype(out[name].dtype))
    for name, factor in factors.items():
        out[name] = (out[name] * factor).astype(out[name].dtype)
    return out
```

```python
from contextlib import ExitStack

import concourse.bass as bass
from concourse import mybir

P = 128
F32 = mybir.dt.float32
BF16 = mybir.dt.bfloat16
I32 = mybir.dt.int32
U32 = mybir.dt.uint32
ALU = mybir.AluOpType
ACT = mybir.ActivationFunctionType
AX_X = mybir.AxisListType.X

B, S, D = 4, 256, 256
TOKENS = B * S
TILES = TOKENS // P
HALVES = S // P
CTX = 64
HEADS = 4
TOP_ROW = int(S * 0.3)
ROUNDS = (TOP_ROW + 7) // 8
E, TOP_E, HID = 12, 3, 640
KT = D // P
HT = HID // P
HALF = HID // 2
SLOTS = (TOP_E * TOKENS + E * (P - 1)) // P
AHEAD = 4
PHI = D // 2
LOWEST = -3.0e38
EPS = 1e-5


def flamingo_block(nc, x, ctx_in, g_xattn, g_ffn, wq, wk, gamma_raw, wr, br, w1, b1, w2, b2,
                   wp1, bp1, wp2, bp2, out):
    assert SLOTS % 2 == 1 and (SLOTS - 3) % AHEAD == 0 and ROUNDS * 8 - TOP_ROW < 8

    normed_rows = nc.dram_tensor("normed_rows", [TOKENS, D], F32).ap()
    expert_sum = nc.dram_tensor("expert_sum", [TOKENS + P, D], F32).ap()

    x_rows = x.rearrange("b s d -> (b s) d").rearrange("(r p) d -> p r d", p=P)
    ctx_rows = ctx_in.rearrange("b s d -> (b s) d").rearrange("(r p) d -> p r d", p=P)
    out_rows = out.rearrange("b s d -> (b s) d").rearrange("(r p) d -> p r d", p=P)

    with ExitStack() as stack:
        def sb(name, shape, dt=F32):
            return stack.enter_context(nc.sbuf_tensor(name, shape, dt))

        def sem(name):
            return stack.enter_context(nc.semaphore(name))

        w1_sb = sb("w1_sb", [P, E, KT, HID])
        w2_sb = sb("w2_sb", [P, E, HT, D])
        b1_bc = sb("b1_bc", [P, E * HID])
        b2_bc = sb("b2_bc", [P, E, D])
        x_sb = sb("x_sb", [P, TILES, D])
        z_sb = x_sb
        x1_sb = sb("x1_sb", [P, TILES, D])
        sim_sb = sb("sim_sb", [P, TILES, D])
        work_sb = sb("work_sb", [P, TILES, D])
        a_sb = sb("a_sb", [P, TILES, D])
        flat = b1_bc[:]
        qT = flat[0:CTX, 0:TOKENS]
        kT = flat[0:CTX, TOKENS:2 * TOKENS]
        cT = flat[0:CTX, 2 * TOKENS:3 * TOKENS]
        ctx_sb = flat[:, 3 * TOKENS:3 * TOKENS + TILES * CTX].rearrange("p (r d) -> p r d", r=TILES)
        wqk_sb = flat[0:CTX, 4 * TOKENS:4 * TOKENS + 2 * CTX].rearrange("p (a d) -> p a d", a=2)
        wqkT = flat[0:CTX, 5 * TOKENS:5 * TOKENS + 2 * CTX].rearrange("p (a d) -> p a d", a=2)
        zT_all = sim_sb[:].rearrange("p r (k t) -> p r k t", k=KT)
        total_sb = sim_sb
        slots_flat = a_sb[:].rearrange("p r d -> p (r d)")
        h_sb = slots_flat[:, 0:HID]
        hT_sb = slots_flat[:, HID:2 * HID].rearrange("p (c t) -> p c t", c=HT)
        rows_sb = sim_sb[:, 0:AHEAD, :]
        zT_sb = slots_flat[:, 2 * HID:2 * HID + D].rearrange("p (k t) -> p k t", k=KT)
        PAIRS = TOP_E * TILES
        row_hot = a_sb[:].rearrange("p r d -> p (r d)")[:, 0:PAIRS * P // 2].bitcast(BF16).rearrange(
            "p (m t) -> p m t", m=PAIRS)
        x_flat = x_sb[:].rearrange("p r d -> p (r d)")
        HOTS = PAIRS * SLOTS
        slot_hot = x_flat[:, 0:HOTS].rearrange("p (m s) -> p m s", m=PAIRS)
        slot_p = x_flat[:, HOTS:HOTS * 3 // 2].bitcast(BF16).rearrange("p (m s) -> p m s", m=PAIRS)
        slot_t = x_flat[:, HOTS * 3 // 2:2 * HOTS].bitcast(BF16).rearrange("p (m s) -> p m s", m=PAIRS)
        y_sb = x_flat[:, 0:2 * D].rearrange("p (n d) -> p n d", n=2)
        used = [0]

        def routing(shape, names):
            n = 1
            for size in shape:
                n *= size
            part = work_sb[:].rearrange("p r d -> p (r d)")[:, used[0]:used[0] + n]
            used[0] += n
            assert used[0] <= TILES * D
            sizes = dict(zip(names.split(), shape))
            first = names.split()[:-1]
            return part.rearrange("p (%s) -> p %s" % (names, names), **{a: sizes[a] for a in first})


        ident = sb("ident", [P, P])
        ones_f = sb("ones_f", [P, P])
        ones_b = sb("ones_b", [P, P], BF16)
        before_b = sb("before_b", [P, P], BF16)
        zeros = sb("zeros", [P, D])
        expert_no = sb("expert_no", [P, E])
        row_no = sb("row_no", [P, P])
        slot_no = sb("slot_no", [P, SLOTS])
        tile_start = sb("tile_start", [P, TILES])
        part_1 = sb("part_1", [P, 1])
        spare_1 = sb("spare_1", [P, 1])
        earlier = sb("earlier", [P, E, E])

        gates = sb("gates", [P, 3])
        gate = sb("gate", [P, 3])
        coef = sb("coef", [P, 3])
        stats = sb("stats", [P, TILES, 6])
        mv = sb("mv", [P, TILES, 2])
        rstd = sb("rstd", [P, TILES])
        var_eps = sb("var_eps", [P, TILES])
        root = sb("root", [P, TILES])
        newton = sb("newton", [P, TILES])
        base_scale = sb("base_scale", [P, TILES])
        base_shift = sb("base_shift", [P, TILES])
        top8 = sb("top8", [P, TILES, 8])
        wr_sb = sb("wr_sb", [P, KT, E])
        br_bc = sb("br_bc", [P, E])
        logits = routing([TILES, E], "r e")
        row_max = sb("row_max", [P, TILES])
        probs = routing([TILES, E], "r e")
        top_p = sb("top_p", [P, TILES, 8])
        top_i = sb("top_i", [P, TILES, 8], U32)
        pick = sb("pick", [P, TILES, TOP_E])
        mix = sb("mix", [P, TILES, TOP_E])
        hot = routing([TOP_E, TILES, E], "k r e")
        hot_x = routing([TOP_E, TILES, E], "k r e")
        chosen = sb("chosen", [P, TILES, E], BF16)
        chosen_w = routing([TILES, E], "r e")
        count = sb("count", [P, E])
        weight = sb("weight", [P, E])
        over = routing([E, TILES], "e r")
        slots_of = sb("slots_of", [P, E])
        before_e = routing([E, E], "e f")
        first_slot = sb("first_slot", [P, E])
        end_slot = sb("end_slot", [P, E])
        slot_expert_f = sb("slot_expert_f", [P, SLOTS])
        slot_expert = sb("slot_expert", [P, SLOTS], I32)
        place = routing([TILES, E], "r e")
        passed = routing([SLOTS, E], "s e")
        pos = sb("pos", [P, PAIRS])
        pos_i = sb("pos_i", [P, 3, PAIRS], I32)
        pos_f = sb("pos_f", [P, 2, PAIRS])
        empty = sb("empty", [P, SLOTS])
        gather_idx = sb("gather_idx", [P, SLOTS], I32)
        scatter_idx = sb("scatter_idx", [P, SLOTS], I32)
        wp1_sb = sb("wp1_sb", [P, KT, PHI])
        bp1_sb = sb("bp1_sb", [P, 1])
        wp2_sb = sb("wp2_sb", [P, 1])
        wp2_bc = row_no
        bp2_bc = sb("bp2_bc", [P, 1])
        mean_w = sb("mean_w", [P, 1])
        pooledT = sb("pooledT", [P, KT, B])
        phi_h = sb("phi_h", [P, B])
        phi = sb("phi", [P, B])
        factor = sb("factor", [P, B])

        ps = stack.enter_context(nc.psum_tensor("ps", [P, 8, 512], F32))
        ctxT_ps = [ps[0:CTX, 0, :], ps[0:CTX, 1, :]]
        wT_ps = ps[0:CTX, 2, 0:2 * CTX].rearrange("p (a d) -> p a d", a=2)
        q_ps = [ps[0:CTX, 3, :], ps[0:CTX, 4, :]]
        k_ps = [ps[0:CTX, 5, :], ps[0:CTX, 6, :]]
        pair_bank = [7, 0, 1, 2]
        sum_bank = [3, 4, 5, 6]
        logits_ps = ps[:, 3, 0:TILES * E]
        rank_ps = ps[:, 4, 0:TILES * E]
        count_ps = ps[:, 5, 0:E]
        mix_ps = ps[:, 6, 0:E]
        token_ps = ps[:, 7, 0:SLOTS]
        hid_ps = ps[:, 0:2, 0:HALF]
        hT_ps = ps[:, 2:4, :].rearrange("p a b -> p (a b)")[:, 0:HID].rearrange("p (c t) -> p c t", c=HT)
        zT_ps = ps[:, 4, 0:D].rearrange("p (k t) -> p k t", k=KT)
        y_ps = ps[:, 5, 0:D]
        pool_ps = ps[:, 7, 0:KT * B].rearrange("p (k b) -> p k b", k=KT)
        phi_h_ps = ps[:, 0, 0:B]
        phi_ps = ps[:, 1, 0:B]

        ctx_loaded = sem("ctx_loaded")
        wqk_loaded = sem("wqk_loaded")
        x_loaded = sem("x_loaded")
        small_loaded = sem("small_loaded")
        weights_loaded = sem("weights_loaded")
        b1_loaded = sem("b1_loaded")
        consts_half = sem("consts_half")
        consts = sem("consts")
        ctxT_done = sem("ctxT_done")
        ctxT_copied = sem("ctxT_copied")
        qk_done = sem("qk_done")
        q_copied = sem("q_copied")
        k_copied = sem("k_copied")
        sims_done = sem("sims_done")
        sims_copied = sem("sims_copied")
        gates_done = sem("gates_done")
        x_step = sem("x_step")
        base_coefs = sem("base_coefs")
        var_ready = sem("var_ready")
        root_done = sem("root_done")
        base_done = sem("base_done")
        sig_done = sem("sig_done")
        topk_step = sem("topk_step")
        masked = sem("masked")
        sym_done = sem("sym_done")
        x1_step = sem("x1_step")
        z_done = sem("z_done")
        z_stored = sem("z_stored")
        zT_done = sem("zT_done")
        zT_copied = sem("zT_copied")
        logits_done = sem("logits_done")
        route_step = sem("route_step")
        shifted = sem("shifted")
        exp_done = sem("exp_done")
        mix_shifted = sem("mix_shifted")
        mix_exp_done = sem("mix_exp_done")
        chosen_done = sem("chosen_done")
        counts_done = sem("counts_done")
        weights_known = sem("weights_known")
        b2_scaled = sem("b2_scaled")
        places_done = sem("places_done")
        tokens_done = sem("tokens_done")
        experts_known = sem("experts_known")
        indices_done = sem("indices_done")
        gathered = [sem("gathered_%d" % n) for n in range(AHEAD)]
        rows_turned = sem("rows_turned")
        rows_copied = sem("rows_copied")
        hidden_done = sem("hidden_done")
        hidden_biased = sem("hidden_biased")
        hidden_turned = sem("hidden_turned")
        hidden_relu = sem("hidden_relu")
        y_done = sem("y_done")
        y_ready = sem("y_ready")
        sum_zeroed = sem("sum_zeroed")
        sum_landed = sem("sum_landed")
        total_loaded = sem("total_loaded")
        wp2_ready = sem("wp2_ready")
        pooled_done = sem("pooled_done")
        pooled_copied = sem("pooled_copied")
        phi_h_done = sem("phi_h_done")
        phi_h_copied = sem("phi_h_copied")
        phi_done = sem("phi_done")
        phi_copied = sem("phi_copied")
        end_step = sem("end_step")
        out_ready = sem("out_ready")
        out_stored = sem("out_stored")
        zeros_ready = sem("zeros_ready")

        block = stack.enter_context(nc.Block())

        @block.sync
        def _(sp):
            sp.dma_start(wqk_sb[:, 0, :], wq).then_inc(wqk_loaded, 16)
            sp.dma_start(wqk_sb[:, 1, :], wk).then_inc(wqk_loaded, 16)
            sp.dma_start(ctx_sb, ctx_rows).then_inc(ctx_loaded, 16)
            sp.dma_start(x_sb[:], x_rows).then_inc(x_loaded, 16)
            for n, g in enumerate((g_xattn, g_ffn, gamma_raw)):
                sp.dma_start(gates[:, n:n + 1], g.rearrange("(a n) -> a n", a=1).to_broadcast([P, 1])
                             ).then_inc(small_loaded, 16)
            sp.dma_start(wr_sb[:], wr.rearrange("(k p) e -> p k e", p=P)).then_inc(small_loaded, 16)
            sp.dma_start(br_bc[:], br.rearrange("(a n) -> a n", a=1).to_broadcast([P, E])
                         ).then_inc(small_loaded, 16)
            sp.dma_start(wp1_sb[:], wp1.rearrange("(k p) j -> p k j", p=P)).then_inc(small_loaded, 16)
            sp.dma_start(bp1_sb[:], bp1.rearrange("(p a) -> p a", a=1)).then_inc(small_loaded, 16)
            sp.dma_start(wp2_sb[:], wp2).then_inc(small_loaded, 16)
            sp.dma_start(bp2_bc[:], bp2.rearrange("(a n) -> a n", a=1).to_broadcast([P, 1])
                         ).then_inc(small_loaded, 16)
            sp.dma_start(b2_bc[:].rearrange("p e d -> p (e d)"),
                         b2.rearrange("e d -> (e d)").rearrange("(a n) -> a n", a=1).to_broadcast([P, E * D])
                         ).then_inc(small_loaded, 16)
            for e in range(E):
                sp.dma_start(w1_sb[:, e], w1[e].rearrange("(k p) i -> p k i", p=P)).then_inc(weights_loaded, 16)
                sp.dma_start(w2_sb[:, e], w2[e].rearrange("(c p) d -> p c d", p=P)).then_inc(weights_loaded, 16)
            sp.wait_ge(zeros_ready, 1)
            sp.dma_start(expert_sum.rearrange("(r p) d -> p r d", p=P),
                         zeros[:].rearrange("p (a d) -> p a d", a=1).to_broadcast([P, TILES + 1, D])
                         ).then_inc(sum_zeroed, 16)
            sp.wait_ge(sims_done, B)
            sp.dma_start(b1_bc[:], b1.rearrange("e i -> (e i)").rearrange("(a n) -> a n", a=1)
                         .to_broadcast([P, E * HID])).then_inc(b1_loaded, 16)
            for r in range(TILES):
                sp.wait_ge(z_done, r + 1)
                sp.dma_start(normed_rows[r * P:(r + 1) * P, :], z_sb[:, r, :]).then_inc(z_stored, 16)
            sp.wait_ge(sum_landed, 16 * SLOTS)
            for b in range(B):
                sp.dma_start(total_sb[:, b * HALVES:(b + 1) * HALVES, :],
                             expert_sum[b * S:(b + 1) * S, :].rearrange("(r p) d -> p r d", p=P)
                             ).then_inc(total_loaded, 16)
            for b in range(B):
                sp.wait_ge(out_ready, b + 1)
                sp.dma_start(out_rows[:, b * HALVES:(b + 1) * HALVES, :],
                             x1_sb[:, b * HALVES:(b + 1) * HALVES, :]).then_inc(out_stored, 16)
            sp.wait_ge(out_stored, 16 * B)

        @block.gpsimd
        def _(pool):
            nc.gpsimd.memset(ident[:], 0.0)
            nc.gpsimd.memset(zeros[:], 0.0).then_inc(zeros_ready, 1)
            nc.gpsimd.memset(before_b[:], 1.0)
            nc.gpsimd.memset(earlier[:], 1.0)
            nc.gpsimd.memset(mean_w[:], 1.0 / S)
            nc.gpsimd.memset(ones_f[:], 1.0)
            nc.gpsimd.memset(ones_b[:], 1.0).then_inc(consts_half, 1)
            pool.wait_ge(consts_half, 1)
            nc.gpsimd.affine_select(out=ident[:], in_=ident[:], compare_op=ALU.not_equal, fill=1.0,
                                    base=0, pattern=[[-1, P]], channel_multiplier=1).then_inc(consts, 1)
            nc.gpsimd.affine_select(out=before_b[:], in_=before_b[:], compare_op=ALU.is_gt, fill=0.0,
                                    base=0, pattern=[[1, P]], channel_multiplier=-1)
            nc.gpsimd.affine_select(out=earlier[:], in_=earlier[:], compare_op=ALU.is_gt, fill=0.0,
                                    base=0, pattern=[[1, E], [-1, E]], channel_multiplier=0)
            exact = dict(allow_small_or_imprecise_dtypes=True)
            nc.gpsimd.iota(expert_no[:], pattern=[[1, E]], base=0, channel_multiplier=0, **exact)
            nc.gpsimd.iota(row_no[:], pattern=[[1, P]], base=0, channel_multiplier=0, **exact)
            nc.gpsimd.iota(slot_no[:], pattern=[[1, SLOTS]], base=0, channel_multiplier=0, **exact)
            nc.gpsimd.iota(tile_start[:], pattern=[[P, TILES]], base=0, channel_multiplier=0, **exact)
            nc.gpsimd.iota(part_1[:], pattern=[[0, 1]], base=1, channel_multiplier=1, **exact)
            nc.gpsimd.iota(spare_1[:], pattern=[[0, 1]], base=TOKENS + 1, channel_multiplier=1,
                           **exact).then_inc(consts, 1)

            def gather(s):
                if s >= AHEAD:
                    pool.wait_ge(rows_turned, s - AHEAD + 1)
                nc.gpsimd.indirect_dma_start(
                    out=rows_sb[:, s % AHEAD, :], out_offset=None, in_=normed_rows[:, :],
                    in_offset=bass.IndirectOffsetOnAxis(ap=gather_idx[:, s:s + 1], axis=0),
                ).then_inc(gathered[s % AHEAD], 16)

            pool.wait_ge(indices_done, 2)
            pool.wait_ge(z_stored, 16 * TILES)
            pool.wait_ge(sum_zeroed, 16)
            for s in range(AHEAD):
                gather(s)
            for s in range(SLOTS):
                if 1 <= s <= SLOTS - AHEAD:
                    gather(s - 1 + AHEAD)
                pool.wait_ge(y_ready, s + 1)
                if s >= 1:
                    pool.wait_ge(sum_landed, 16 * s)
                nc.gpsimd.indirect_dma_start(
                    out=expert_sum[:, :],
                    out_offset=bass.IndirectOffsetOnAxis(ap=scatter_idx[:, s:s + 1], axis=0),
                    in_=y_sb[:, s % 2, :], in_offset=None, compute_op=ALU.add,
                ).then_inc(sum_landed, 16)

        @block.tensor
        def _(pe):
            pe.wait_ge(consts, 1)
            pe.wait_ge(wqk_loaded, 32)
            for a in range(2):
                nc.tensor.transpose(wT_ps[:, a, :], wqk_sb[:, a, :], ident[0:CTX, 0:CTX])
            pe.wait_ge(ctx_loaded, 16)
            for r in range(TILES):
                turned = nc.tensor.transpose(ctxT_ps[r // 4][:, (r % 4) * P:(r % 4 + 1) * P], ctx_sb[:, r, :],
                                             ident[:])
                if r % 4 == 3:
                    turned.then_inc(ctxT_done, 1)
            for half in range(2):
                pe.wait_ge(ctxT_copied, half + 2)
                for a, to in enumerate((q_ps, k_ps)):
                    nc.tensor.matmul(to[half], wqkT[:, a, :], cT[:, half * 512:(half + 1) * 512],
                                     start=True, stop=True).then_inc(qk_done, 1)
            for b in range(B):
                pe.wait_ge(q_copied, b // 2 + 1)
                pe.wait_ge(k_copied, b // 2 + 1)
                for half in range(HALVES):
                    r = b * HALVES + half
                    last = nc.tensor.matmul(ps[:, pair_bank[b], half * S:(half + 1) * S], qT[:, r * P:(r + 1) * P],
                                            kT[:, b * S:(b + 1) * S], start=True, stop=True)
                last.then_inc(sims_done, 1)
            for b in range(B):
                pe.wait_ge(masked, (b + 1) * HALVES)
                for half in range(HALVES):
                    to = ps[:, sum_bank[b], half * S:(half + 1) * S]
                    nc.tensor.matmul(to, ident[:], a_sb[:, b * HALVES + half, :], start=True, stop=False)
                    for j in range(HALVES):
                        last = nc.tensor.matmul(to[:, j * P:(j + 1) * P],
                                                a_sb[:, b * HALVES + j, half * P:(half + 1) * P], ident[:],
                                                start=False, stop=(j == HALVES - 1))
                last.then_inc(sym_done, 1)
            for b in range(B):
                pe.wait_ge(sims_copied, 2 * (b + 1))
                for half in range(HALVES):
                    r = b * HALVES + half
                    pe.wait_ge(z_done, r + 1)
                    for k in range(KT):
                        col = half * D + k * P
                        last = nc.tensor.transpose(ps[:, pair_bank[b], col:col + P], z_sb[:, r, k * P:(k + 1) * P],
                                                   ident[:])
                last.then_inc(zT_done, 1)
            pe.wait_ge(small_loaded, 160)
            for r in range(TILES):
                pe.wait_ge(zT_copied, r // HALVES + 1)
                for k in range(KT):
                    last = nc.tensor.matmul(logits_ps[:, r * E:(r + 1) * E], zT_all[:, r, k, :], wr_sb[:, k, :],
                                            start=(k == 0), stop=(k == KT - 1))
            last.then_inc(logits_done, 1)
            pe.wait_ge(chosen_done, 1)
            pe.wait_ge(consts, 2)
            for j in range(TILES):
                last = nc.tensor.matmul(count_ps, ones_b[:], chosen[:, j, :], start=(j == 0), stop=(j == TILES - 1))
            last.then_inc(counts_done, 1)
            chosen_flat = chosen[:].rearrange("p r e -> p (r e)")
            nc.tensor.matmul(rank_ps, before_b[:], chosen_flat, start=True, stop=False)
            for j in range(TILES - 1):
                later = TILES - 1 - j
                last = nc.tensor.matmul(
                    rank_ps[:, (j + 1) * E:].rearrange("p (r e) -> p r e", e=E), ones_b[:],
                    chosen[:, j:j + 1, :].to_broadcast([P, later, E]), start=False, stop=(j == TILES - 2))
            last.then_inc(counts_done, 1)
            pe.wait_ge(chosen_done, 2)
            for j in range(TILES):
                last = nc.tensor.matmul(mix_ps, ones_f[:], chosen_w[:, j, :], start=(j == 0), stop=(j == TILES - 1))
            last.then_inc(counts_done, 1)
            pe.wait_ge(places_done, 3)
            for m in range(PAIRS):
                nc.tensor.matmul(token_ps, row_hot[:, m, :], slot_p[:, m, :], start=(m == 0), stop=False)
                last = nc.tensor.matmul(token_ps, row_hot[:, m, :], slot_t[:, m, :], start=False,
                                        stop=(m == PAIRS - 1))
            last.then_inc(tokens_done, 1)

            def turn_rows(s, buf, nth):
                pe.wait_ge(gathered[buf], nth * 16 + 16)
                for k in range(KT):
                    last = nc.tensor.transpose(zT_ps[:, k, :], rows_sb[:, buf, k * P:(k + 1) * P], ident[:])
                last.then_inc(rows_turned, 1)

            def first_product(s, e):
                pe.wait_ge(rows_copied, s + 1)
                for k in range(KT):
                    for n in range(2):
                        last = nc.tensor.matmul(
                            hid_ps[:, n, :], zT_sb[:, k, :],
                            w1_flat[:, bass.ds(e * (KT * HID) + (k * HID + n * HALF), HALF)],
                            start=(k == 0), stop=(k == KT - 1), skip_group_check=True)
                last.then_inc(hidden_done, 1)

            def turn_hidden(s):
                pe.wait_ge(hidden_biased, s + 1)
                for c in range(HT):
                    last = nc.tensor.transpose(hT_ps[:, c, :], h_sb[:, c * P:(c + 1) * P], ident[:])
                last.then_inc(hidden_turned, 1)

            def second_product(s, e):
                pe.wait_ge(hidden_relu, s + 1)
                if not isinstance(s, int) or s >= 1:
                    pe.wait_ge(y_ready, s)
                for c in range(HT):
                    last = nc.tensor.matmul(y_ps, hT_sb[:, c, :], w2_flat[:, bass.ds(e * (HT * D) + c * D, D)],
                                            start=(c == 0), stop=(c == HT - 1))
                last.then_inc(y_done, 1)

            w1_flat = w1_sb[:].rearrange("p e k i -> p (e k i)")
            w2_flat = w2_sb[:].rearrange("p e c d -> p (e c d)")

            def expert_of(s):
                return pe.value_load(slot_expert[0:1, bass.ds(s, 1)], min_val=0, max_val=E - 1)

            pe.wait_ge(experts_known, 1)
            pe.wait_ge(weights_loaded, 32 * E)
            turn_rows(0, 0, 0)
            first_product(0, expert_of(0))
            turn_rows(1, 1, 0)
            turn_hidden(0)

            def step(s, buf, nth):
                first_product(s, expert_of(s))
                turn_rows(s + 1, buf, nth)
                second_product(s - 1, expert_of(s - 1))
                turn_hidden(s)

            step(1, 2 % AHEAD, 2 // AHEAD)
            with pe.Fori(0, (SLOTS - 3) // AHEAD) as i:
                for j in range(AHEAD):
                    step(i * AHEAD + 2 + j, (3 + j) % AHEAD, i + (3 + j) // AHEAD)
            first_product(SLOTS - 1, expert_of(SLOTS - 1))
            second_product(SLOTS - 2, expert_of(SLOTS - 2))
            turn_hidden(SLOTS - 1)
            second_product(SLOTS - 1, expert_of(SLOTS - 1))

            for b in range(B):
                pe.wait_ge(total_loaded, 16 * B)
                for k in range(KT):
                    for half in range(HALVES):
                        last = nc.tensor.matmul(pool_ps[:, k, b:b + 1],
                                                total_sb[:, b * HALVES + half, k * P:(k + 1) * P], mean_w[:],
                                                start=(half == 0), stop=(half == HALVES - 1))
            last.then_inc(pooled_done, 1)
            pe.wait_ge(pooled_copied, 1)
            for k in range(KT):
                last = nc.tensor.matmul(phi_h_ps, wp1_sb[:, k, :], pooledT[:, k, :], start=(k == 0),
                                        stop=(k == KT - 1))
            last.then_inc(phi_h_done, 1)
            pe.wait_ge(phi_h_copied, 1)
            pe.wait_ge(wp2_ready, 1)
            nc.tensor.matmul(phi_ps, wp2_bc[:], phi_h[:], start=True, stop=True).then_inc(phi_done, 1)

        @block.scalar
        def _(act):
            scale = 1.0 / ((CTX // HEADS) ** 0.5 * HEADS)
            act.wait_ge(ctxT_done, 1)
            nc.scalar.copy(wqkT, wT_ps).then_inc(ctxT_copied, 1)
            for half in range(2):
                act.wait_ge(ctxT_done, half + 1)
                nc.scalar.copy(cT[:, half * 512:(half + 1) * 512], ctxT_ps[half]).then_inc(ctxT_copied, 1)
            for half in range(2):
                act.wait_ge(qk_done, 2 * half + 1)
                nc.scalar.mul(qT[:, half * 512:(half + 1) * 512], q_ps[half], scale).then_inc(q_copied, 1)
            for b in range(B):
                act.wait_ge(sims_done, b + 1)
                bank = ps[:, pair_bank[b], :].rearrange("p (h s) -> p h s", h=HALVES)
                nc.scalar.copy(work_sb[:, b * HALVES:(b + 1) * HALVES, :], bank).then_inc(sims_copied, 1)
                nc.scalar.copy(sim_sb[:, b * HALVES:(b + 1) * HALVES, :], bank).then_inc(sims_copied, 1)
            act.wait_ge(small_loaded, 160)
            nc.scalar.activation(gate[:, 0:2], gates[:, 0:2], ACT.Tanh).then_inc(gates_done, 1)
            nc.scalar.activation(gate[:, 2:3], gates[:, 2:3], ACT.Sigmoid).then_inc(gates_done, 1)
            for b in range(B):
                act.wait_ge(sims_copied, 2 * b + 2)
                nc.scalar.activation(a_sb[:, b * HALVES:(b + 1) * HALVES, :],
                                     sim_sb[:, b * HALVES:(b + 1) * HALVES, :], ACT.Sigmoid).then_inc(sig_done, 1)
            act.wait_ge(var_ready, 1)
            nc.scalar.activation(root[:], var_eps[:], ACT.Sqrt).then_inc(root_done, 1)
            act.wait_ge(base_coefs, 1)
            for r in range(TILES):
                nc.scalar.activation(x1_sb[:, r, :], x_sb[:, r, :], ACT.Identity, bias=base_shift[:, r:r + 1],
                                     scale=base_scale[:, r:r + 1]).then_inc(base_done, 1)
            act.wait_ge(var_ready, 2)
            nc.scalar.activation(root[:], var_eps[:], ACT.Sqrt).then_inc(root_done, 1)
            for b in range(B):
                act.wait_ge(zT_done, b + 1)
                nc.scalar.copy(sim_sb[:, b * HALVES:(b + 1) * HALVES, :],
                               ps[:, pair_bank[b], :].rearrange("p (h s) -> p h s", h=HALVES)
                               ).then_inc(zT_copied, 1)
            act.wait_ge(shifted, 1)
            nc.scalar.activation(probs, logits, ACT.Exp).then_inc(exp_done, 1)
            act.wait_ge(mix_shifted, 1)
            nc.scalar.activation(mix[:], mix[:], ACT.Exp).then_inc(mix_exp_done, 1)
            act.wait_ge(weights_known, 1)
            for e in range(E):
                nc.scalar.activation(b2_bc[:, e, :], b2_bc[:, e, :], ACT.Copy, scale=weight[:, e:e + 1]
                                     ).then_inc(b2_scaled, 1)

            def copy_rows(s):
                act.wait_ge(rows_turned, s + 1)
                nc.scalar.copy(zT_sb, zT_ps).then_inc(rows_copied, 1)

            def relu_hidden(s):
                act.wait_ge(hidden_turned, s + 1)
                nc.scalar.activation(hT_sb, hT_ps, ACT.Relu).then_inc(hidden_relu, 1)

            copy_rows(0)
            with act.Fori(0, SLOTS - 1) as s:
                copy_rows(s + 1)
                relu_hidden(s)
            relu_hidden(SLOTS - 1)

            act.wait_ge(phi_h_done, 1)
            nc.scalar.activation(phi_h[:], phi_h_ps, ACT.Relu, bias=bp1_sb[:]).then_inc(phi_h_copied, 1)
            act.wait_ge(phi_done, 1)
            nc.scalar.activation(phi[:], phi_ps, ACT.Sigmoid, bias=bp2_bc[:]).then_inc(phi_copied, 1)

        @block.vector
        def _(dve):
            for half in range(2):
                dve.wait_ge(qk_done, 2 * half + 2)
                nc.vector.tensor_copy(kT[:, half * 512:(half + 1) * 512], k_ps[half]).then_inc(k_copied, 1)

            def row_stats(rows, nth, step, before, waits):
                for r in range(TILES):
                    waits(r)
                    nc.vector.bn_stats(stats[:, r, :], rows[:, r, :]).then_inc(step, 1)
                for r in range(TILES):
                    dve.wait_ge(step, before + r + 1)
                    nc.vector.bn_aggr(mv[:, r, :], stats[:, r, :]).then_inc(step, 1)
                n = before + 2 * TILES
                dve.wait_ge(step, n)
                nc.vector.tensor_scalar_add(var_eps[:], mv[:, :, 1], EPS).then_inc(var_ready, 1)
                dve.wait_ge(root_done, nth)
                nc.vector.reciprocal(rstd[:], root[:]).then_inc(step, 1)
                dve.wait_ge(step, n + 1)
                nc.vector.tensor_mul(newton[:], rstd[:], rstd[:]).then_inc(step, 1)
                dve.wait_ge(step, n + 2)
                nc.vector.tensor_mul(newton[:], newton[:], var_eps[:]).then_inc(step, 1)
                dve.wait_ge(step, n + 3)
                nc.vector.tensor_scalar(newton[:], newton[:], -0.5, 1.5, ALU.mult, ALU.add).then_inc(step, 1)
                dve.wait_ge(step, n + 4)
                nc.vector.tensor_mul(rstd[:], rstd[:], newton[:]).then_inc(step, 1)
                dve.wait_ge(step, n + 5)
                return n + 5

            dve.wait_ge(x_loaded, 16)
            n = row_stats(x_sb, 1, x_step, 0, lambda r: None)
            dve.wait_ge(gates_done, 2)
            nc.vector.tensor_mul(coef[:, 0:1], gate[:, 0:1], gate[:, 2:3]).then_inc(x_step, 1)
            dve.wait_ge(x_step, n + 1)
            nc.vector.tensor_sub(coef[:, 1:2], gate[:, 0:1], coef[:, 0:1]).then_inc(x_step, 1)
            nc.vector.tensor_scalar_mul(coef[:, 2:3], coef[:, 0:1], 0.5)
            nc.vector.tensor_mul(base_shift[:], rstd[:], mv[:, :, 0]).then_inc(x_step, 1)
            dve.wait_ge(x_step, n + 3)
            nc.vector.tensor_scalar(base_scale[:], rstd[:], coef[:, 1:2], 1.0, ALU.mult, ALU.add)
            nc.vector.tensor_scalar(base_shift[:], base_shift[:], coef[:, 1:2], -1.0, ALU.mult, ALU.mult
                                    ).then_inc(base_coefs, 1)

            for r in range(TILES):
                dve.wait_ge(sims_copied, 2 * (r // HALVES) + 1)
                nc.vector.max(top8[:, r, :], work_sb[:, r, :]).then_inc(topk_step, 1)
            for j in range(ROUNDS - 1):
                for r in range(TILES):
                    dve.wait_ge(topk_step, j * 2 * TILES + r + 1)
                    nc.vector.match_replace(work_sb[:, r, :], top8[:, r, :], work_sb[:, r, :], LOWEST
                                            ).then_inc(topk_step, 1)
                for r in range(TILES):
                    dve.wait_ge(topk_step, j * 2 * TILES + TILES + r + 1)
                    nc.vector.max(top8[:, r, :], work_sb[:, r, :]).then_inc(topk_step, 1)
            last_col = TOP_ROW - 1 - 8 * (ROUNDS - 1)
            for r in range(TILES):
                dve.wait_ge(topk_step, (ROUNDS - 1) * 2 * TILES + r + 1)
                dve.wait_ge(sig_done, r // HALVES + 1)
                nc.vector.scalar_tensor_tensor(
                    out=a_sb[:, r, :], in0=sim_sb[:, r, :], scalar=top8[:, r, last_col:last_col + 1],
                    in1=a_sb[:, r, :], op0=ALU.is_ge, op1=ALU.mult).then_inc(masked, 1)
            for b in range(B):
                dve.wait_ge(sym_done, b + 1)
                dve.wait_ge(base_done, (b + 1) * HALVES)
                rows = x1_sb[:, b * HALVES:(b + 1) * HALVES, :]
                nc.vector.scalar_tensor_tensor(
                    out=rows, in0=ps[:, sum_bank[b], :].rearrange("p (h s) -> p h s", h=HALVES),
                    scalar=coef[:, 2:3], in1=rows, op0=ALU.mult, op1=ALU.add).then_inc(x1_step, 1)
            row_stats(x1_sb, 2, x1_step, B, lambda r: dve.wait_ge(x1_step, r // HALVES + 1))
            for r in range(TILES):
                nc.vector.tensor_scalar(z_sb[:, r, :], x1_sb[:, r, :], mv[:, r, 0:1], rstd[:, r:r + 1],
                                        ALU.subtract, ALU.mult).then_inc(z_done, 1)

            steps = [0]

            def landed(instruction):
                steps[0] += 1
                instruction.then_inc(route_step, 1)
                dve.wait_ge(route_step, steps[0])


            tiles_e = [P, TILES, E]
            dve.wait_ge(consts, 2)
            dve.wait_ge(logits_done, 1)
            landed(nc.vector.tensor_add(
                logits, logits_ps.rearrange("p (r e) -> p r e", e=E),
                br_bc[:].rearrange("p (a e) -> p a e", a=1).to_broadcast(tiles_e)))
            landed(nc.vector.reduce_max(row_max[:], logits, AX_X))
            row_all = row_max[:].rearrange("p (r a) -> p r a", a=1).to_broadcast(tiles_e)
            nc.vector.tensor_sub(logits, logits, row_all).then_inc(shifted, 1)
            dve.wait_ge(exp_done, 1)
            landed(nc.vector.reduce_sum(row_max[:], probs, AX_X))
            landed(nc.vector.reciprocal(row_max[:], row_max[:]))
            landed(nc.vector.tensor_mul(probs, probs, row_all))
            for r in range(TILES):
                largest = nc.vector.max(top_p[:, r, :], probs[:, r, :])
            landed(largest)
            for r in range(TILES):
                where = nc.vector.max_index(top_i[:, r, :], top_p[:, r, :], probs[:, r, :])
            tiles_k = [P, TILES, TOP_E]
            nc.vector.tensor_sub(mix[:], top_p[:, :, 0:TOP_E], top_p[:, :, 0:1].to_broadcast(tiles_k)
                                 ).then_inc(mix_shifted, 1)
            landed(where)
            landed(nc.vector.tensor_copy(pick[:], top_i[:, :, 0:TOP_E]))
            hot_shape = [P, TOP_E, TILES, E]
            for k in range(TOP_E):
                made = nc.vector.tensor_tensor(
                    hot[:, k], expert_no[:].rearrange("p (a e) -> p a e", a=1).to_broadcast(tiles_e),
                    pick[:, :, k:k + 1].to_broadcast(tiles_e), ALU.is_equal)
            landed(made)
            with nc.allow_low_precision("sums of at most three zeros and ones"):
                nc.vector.tensor_reduce(chosen[:], hot.rearrange("p k r e -> p r e k"), AX_X, ALU.add
                                        ).then_inc(chosen_done, 1)
            dve.wait_ge(mix_exp_done, 1)
            landed(nc.vector.reduce_sum(row_max[:], mix[:], AX_X))
            landed(nc.vector.reciprocal(row_max[:], row_max[:]))
            landed(nc.vector.tensor_mul(mix[:], mix[:], row_max[:].rearrange("p (r a) -> p r a", a=1)
                                        .to_broadcast(tiles_k)))
            for k in range(TOP_E):
                made = nc.vector.tensor_mul(hot_x[:, k], hot[:, k], mix[:, :, k:k + 1].to_broadcast(tiles_e))
            landed(made)
            nc.vector.tensor_reduce(chosen_w[:], hot_x.rearrange("p k r e -> p r e k"), AX_X, ALU.add
                                    ).then_inc(chosen_done, 1)
            dve.wait_ge(counts_done, 1)
            landed(nc.vector.tensor_copy(count[:], count_ps))
            landed(nc.vector.tensor_tensor(
                over, count[:].rearrange("p (e a) -> p e a", a=1).to_broadcast([P, E, TILES]),
                tile_start[:].rearrange("p (a r) -> p a r", a=1).to_broadcast([P, E, TILES]), ALU.is_gt))
            landed(nc.vector.reduce_sum(slots_of[:], over, AX_X))
            landed(nc.vector.tensor_mul(before_e, earlier[:], slots_of[:].rearrange("p (a e) -> p a e", a=1)
                                        .to_broadcast([P, E, E])))
            landed(nc.vector.reduce_sum(first_slot[:], before_e, AX_X))
            dve.wait_ge(counts_done, 2)
            landed(nc.vector.scalar_tensor_tensor(
                out=place, in0=first_slot[:].rearrange("p (a e) -> p a e", a=1).to_broadcast(tiles_e),
                scalar=float(P), in1=rank_ps.rearrange("p (r e) -> p r e", e=E), op0=ALU.mult, op1=ALU.add))
            for k in range(TOP_E):
                made = nc.vector.tensor_mul(hot_x[:, k], hot[:, k], place)
            landed(made)
            landed(nc.vector.reduce_sum(pos[:], hot_x.rearrange("p k r e -> p (k r) e"), AX_X))
            landed(nc.vector.tensor_copy(pos_i[:, 0, :], pos[:]))
            nc.vector.tensor_single_scalar(pos_i[:, 1, :], pos_i[:, 0, :], 7, ALU.arith_shift_right)
            landed(nc.vector.tensor_single_scalar(pos_i[:, 2, :], pos_i[:, 0, :], P - 1, ALU.bitwise_and))
            landed(nc.vector.tensor_copy(pos_f[:], pos_i[:, 1:3, :]))
            nc.vector.tensor_tensor(row_hot, row_no[:].rearrange("p (a t) -> p a t", a=1)
                                    .to_broadcast([P, PAIRS, P]),
                                    pos_f[:, 1, :].rearrange("p (m a) -> p m a", a=1).to_broadcast([P, PAIRS, P]),
                                    ALU.is_equal).then_inc(places_done, 1)
            pair_slots = [P, PAIRS, SLOTS]
            dve.wait_ge(z_stored, 16 * TILES)
            landed(nc.vector.tensor_tensor(
                slot_hot, slot_no[:].rearrange("p (a s) -> p a s", a=1).to_broadcast(pair_slots),
                pos_f[:, 0, :].rearrange("p (m a) -> p m a", a=1).to_broadcast(pair_slots), ALU.is_equal))
            nc.vector.tensor_scalar(slot_p, slot_hot, part_1[:], None, ALU.mult).then_inc(places_done, 1)
            for k in range(TOP_E):
                made = nc.vector.tensor_mul(
                    slot_t[:, k * TILES:(k + 1) * TILES, :], slot_hot[:, k * TILES:(k + 1) * TILES, :],
                    tile_start[:].rearrange("p (r a) -> p r a", a=1).to_broadcast([P, TILES, SLOTS]))
            made.then_inc(places_done, 1)
            landed(nc.vector.tensor_add(end_slot[:], first_slot[:], slots_of[:]))
            slot_e = [P, SLOTS, E]
            landed(nc.vector.tensor_tensor(
                passed, slot_no[:].rearrange("p (s a) -> p s a", a=1).to_broadcast(slot_e),
                end_slot[:].rearrange("p (a e) -> p a e", a=1).to_broadcast(slot_e), ALU.is_ge))
            landed(nc.vector.reduce_sum(slot_expert_f[:], passed, AX_X))
            nc.vector.tensor_scalar(slot_expert[:], slot_expert_f[:], float(E - 1), None, ALU.min).then_inc(
                experts_known, 1)
            dve.wait_ge(counts_done, 3)
            landed(nc.vector.tensor_scalar(count[:], count[:], 1.0, None, ALU.max))
            landed(nc.vector.reciprocal(count[:], count[:]))
            nc.vector.tensor_mul(weight[:], mix_ps, count[:]).then_inc(weights_known, 1)
            dve.wait_ge(tokens_done, 1)
            nc.vector.tensor_scalar(gather_idx[:], token_ps, -1.0, 0.0, ALU.add, ALU.max).then_inc(indices_done, 1)
            landed(nc.vector.tensor_scalar(empty[:], token_ps, 0.0, spare_1[:], ALU.is_equal, ALU.mult))
            nc.vector.scalar_tensor_tensor(out=scatter_idx[:], in0=token_ps, scalar=-1.0, in1=empty[:],
                                           op0=ALU.add, op1=ALU.add).then_inc(indices_done, 1)

            def bias_hidden(s, e):
                dve.wait_ge(hidden_done, s + 1)
                nc.vector.tensor_tensor(
                    h_sb.rearrange("p (n i) -> p n i", n=2), hid_ps,
                    b1_bc[:, bass.ds(e * HID, HID)].rearrange("p (n i) -> p n i", n=2), ALU.add
                ).then_inc(hidden_biased, 1)

            def finish_slot(s, odd, e):
                dve.wait_ge(y_done, s + 1)
                if not isinstance(s, int) or s >= 2:
                    dve.wait_ge(sum_landed, s * 16 - 16)
                nc.vector.scalar_tensor_tensor(
                    out=y_sb[:, odd, :], in0=y_ps, scalar=weight[:, bass.ds(e, 1)],
                    in1=b2_flat[:, bass.ds(e * D, D)], op0=ALU.mult, op1=ALU.add).then_inc(y_ready, 1)

            b2_flat = b2_bc[:].rearrange("p e d -> p (e d)")

            def expert_of(s):
                return dve.value_load(slot_expert[0:1, bass.ds(s, 1)], min_val=0, max_val=E - 1)

            dve.wait_ge(b1_loaded, 16)
            dve.wait_ge(experts_known, 1)
            dve.wait_ge(b2_scaled, E)
            bias_hidden(0, expert_of(0))

            def step(s, odd):
                bias_hidden(s, expert_of(s))
                finish_slot(s - 1, odd, expert_of(s - 1))

            step(1, 0)
            step(2, 1)
            with dve.Fori(1, (SLOTS - 1) // 2) as i:
                step(i * 2 + 1, 0)
                step(i * 2 + 2, 1)
            finish_slot(SLOTS - 1, 0, expert_of(SLOTS - 1))

            nc.vector.tensor_scalar(wp2_bc[:], ones_f[:], wp2_sb[:], None, ALU.mult).then_inc(wp2_ready, 1)
            dve.wait_ge(pooled_done, 1)
            nc.vector.tensor_copy(pooledT[:], pool_ps).then_inc(pooled_copied, 1)
            dve.wait_ge(phi_copied, 1)
            nc.vector.tensor_scalar(factor[:], phi[:], 0.7, -0.8, ALU.is_gt, ALU.mult).then_inc(end_step, 1)
            dve.wait_ge(end_step, 1)
            nc.vector.tensor_scalar(factor[:], factor[:], 1.0, gate[:, 1:2], ALU.add, ALU.mult).then_inc(end_step, 1)
            dve.wait_ge(end_step, 2)
            for b in range(B):
                rows = x1_sb[:, b * HALVES:(b + 1) * HALVES, :]
                nc.vector.scalar_tensor_tensor(
                    out=rows, in0=total_sb[:, b * HALVES:(b + 1) * HALVES, :], scalar=factor[:, b:b + 1],
                    in1=rows, op0=ALU.mult, op1=ALU.add).then_inc(out_ready, 1)


_INS = ["x", "ctx_512", "g_xattn", "g_ffn", "L0_xattn_Wq", "L0_xattn_Wk", "L0_xattn_gamma_raw", "L0_ffn_Wr",
        "L0_ffn_br", "L0_ffn_w1", "L0_ffn_b1", "L0_ffn_w2", "L0_ffn_b2", "L0_ffn_Wp1", "L0_ffn_bp1",
        "L0_ffn_Wp2", "L0_ffn_bp2"]


def kernel(**inputs):
    import numpy as _np
    import concourse.bacc as _bacc
    from concourse import mybir as _mybir
    from concourse.bass_utils import run_bass_kernel_spmd as _run

    nc = _bacc.Bacc("TRN2", target_bir_lowering=False, num_devices=1, dynamic_dma_scratch_size=8192)
    arrays, args = {}, []
    for name in _INS:
        a = _np.ascontiguousarray(inputs[name])
        arrays[f"in_{name}_dram"] = a
        args.append(nc.dram_tensor(f"in_{name}_dram", a.shape, _mybir.dt.from_np(a.dtype), kind="ExternalInput").ap())
    out = nc.dram_tensor("out_0_dram", (B, S, D), _mybir.dt.float32, kind="ExternalOutput").ap()
    flamingo_block(nc, *args, out)
    r = _run(nc, [arrays], core_ids=[0])
    return r.results[0]["out_0_dram"]
```

```python
from contextlib import ExitStack

import concourse.bass as bass
from concourse import mybir

P = 128
F32 = mybir.dt.float32
BF16 = mybir.dt.bfloat16
F16 = mybir.dt.float16
I32 = mybir.dt.int32
U32 = mybir.dt.uint32
ALU = mybir.AluOpType
ACT = mybir.ActivationFunctionType
AX_X = mybir.AxisListType.X

B, S, D = 4, 256, 256
TOKENS = B * S
TILES = TOKENS // P
HALVES = S // P
CTX = 64
HEADS = 4
TOP_ROW = int(S * 0.3)
ROUNDS = (TOP_ROW + 7) // 8
LAST_COL = TOP_ROW - 1 - 8 * (ROUNDS - 1)
E, TOP_E, HID = 12, 3, 640
KT = D // P
HT = HID // P
SLOTS = (TOP_E * TOKENS + E * (P - 1)) // P
AHEAD = 4
PHI = D // 2
LOWEST = -3.0e38
EPS = 1e-5


def flamingo_block(nc, x, ctx_in, g_xattn, g_ffn, wq, wk, gamma_raw, wr, br, w1, b1, w2, b2,
                   wp1, bp1, wp2, bp2, out):
    assert HALVES == 2 and SLOTS % 2 == 1 and (SLOTS - 3) % AHEAD == 0 and ROUNDS * 8 - TOP_ROW < 8

    normed_rows = nc.dram_tensor("normed_rows", [TOKENS, D], F32).ap()
    expert_sum = nc.dram_tensor("expert_sum", [TOKENS + P, D], F32).ap()

    x_rows = x.rearrange("b s d -> (b s) d").rearrange("(r p) d -> p r d", p=P)
    ctx_rows = ctx_in.rearrange("b s d -> (b s) d").rearrange("(r p) d -> p r d", p=P)
    out_rows = out.rearrange("b s d -> (b s) d").rearrange("(r p) d -> p r d", p=P)

    with ExitStack() as stack:
        def sb(name, shape, dt=F32):
            return stack.enter_context(nc.sbuf_tensor(name, shape, dt))

        def sem(name):
            return stack.enter_context(nc.semaphore(name))

        w1_sb = sb("w1_sb", [P, E, KT, HID])
        w2_sb = sb("w2_sb", [P, E, HT, D])
        slot_w1 = sb("slot_w1", [P, 2, KT * HID])
        b1_rows = sb("b1_rows", [E * HT, P])
        b1T = sb("b1T", [P, E * HT])
        b2_bc = sb("b2_bc", [P, E * D])
        x_sb = sb("x_sb", [P, TILES, D])
        z_sb = x_sb
        x1_sb = sb("x1_sb", [P, TILES, D])
        zT_all = sb("zT_all", [P, TILES, KT, P])
        work_sb = sb("work_sb", [P, TILES, D])
        a_sb = sb("a_sb", [P, TILES, D])
        flat = sb("shared", [P, 2 * TOKENS + TILES * CTX + 3 * CTX])[:]
        cT = flat[0:CTX, 0:TOKENS]
        gT = flat[0:CTX, TOKENS:2 * TOKENS]
        ctx_sb = flat[:, 2 * TOKENS:2 * TOKENS + TILES * CTX].rearrange("p (r d) -> p r d", r=TILES)
        wqk_sb = flat[0:CTX, 2 * TOKENS + TILES * CTX:][:, 0:2 * CTX].rearrange("p (a d) -> p a d", a=2)
        wqk_product = flat[0:CTX, 2 * TOKENS + TILES * CTX:][:, 2 * CTX:3 * CTX]
        hT_sb = flat[:, 0:2 * HID].rearrange("p (n c t) -> p n c t", n=2, c=HT)
        zT_sb = flat[:, 2 * HID:2 * HID + D].rearrange("p (k t) -> p k t", k=KT)
        y_sb = flat[:, 2 * HID + D:2 * HID + 3 * D].rearrange("p (n d) -> p n d", n=2)
        both_halves = slot_w1[:, 0, 0:B * D].rearrange("p (b d) -> p b d", b=B)
        total_sb = zT_all[:].rearrange("p r k t -> p r (k t)")
        sim_sb = total_sb
        rows_sb = total_sb[:, 0:AHEAD, :]
        PAIRS = TOP_E * TILES
        row_hot = a_sb[:].rearrange("p r d -> p (r d)")[:, 0:PAIRS * P // 2].bitcast(F16).rearrange(
            "p (m t) -> p m t", m=PAIRS)
        slot_hot = sb("slot_hot", [P, PAIRS, SLOTS], F16)
        slot_token = sb("slot_token", [P, PAIRS, SLOTS], F16)
        used = [0]

        def routing(shape, names):
            n = 1
            for size in shape:
                n *= size
            part = work_sb[:].rearrange("p r d -> p (r d)")[:, used[0]:used[0] + n]
            used[0] += n
            assert used[0] <= TILES * D
            sizes = dict(zip(names.split(), shape))
            first = names.split()[:-1]
            return part.rearrange("p (%s) -> p %s" % (names, names), **{a: sizes[a] for a in first})


        ident = sb("ident", [P, P])
        ones_f = sb("ones_f", [P, P])
        ones_b = sb("ones_b", [P, P], BF16)
        before_b = sb("before_b", [P, P], BF16)
        zeros = sb("zeros", [P, D])
        expert_no = sb("expert_no", [P, E])
        row_no = sb("row_no", [P, P], F16)
        slot_no_h = sb("slot_no_h", [P, SLOTS], F16)
        slot_no = sb("slot_no", [P, SLOTS])
        tile_start = sb("tile_start", [P, TILES])
        token_1 = sb("token_1", [P, TILES])
        spare_1 = sb("spare_1", [P, 1])
        earlier = sb("earlier", [P, E, E])

        gates = sb("gates", [P, 3])
        gate = sb("gate", [P, 3])
        coef = sb("coef", [P, 3])
        stats = sb("stats", [P, TILES, 6])
        mv = sb("mv", [P, TILES, 2])
        rstd = sb("rstd", [P, TILES])
        var_eps = sb("var_eps", [P, TILES])
        root = sb("root", [P, TILES])
        newton = sb("newton", [P, TILES])
        shift = sb("shift", [P, TILES])
        base_scale = sb("base_scale", [P, TILES])
        base_shift = sb("base_shift", [P, TILES])
        top8 = sb("top8", [P, TILES, 8])
        wr_sb = sb("wr_sb", [P, KT, E])
        br_bc = sb("br_bc", [P, E])
        logits = routing([TILES, E], "r e")
        row_max = sb("row_max", [P, TILES])
        probs = routing([TILES, E], "r e")
        top_p = sb("top_p", [P, TILES, 8])
        top_i = sb("top_i", [P, TILES, 8], U32)
        pick = sb("pick", [P, TILES, TOP_E])
        mix = sb("mix", [P, TILES, TOP_E])
        hot = routing([TOP_E, TILES, E], "k r e")
        hot_x = routing([TOP_E, TILES, E], "k r e")
        chosen = sb("chosen", [P, TILES, E], BF16)
        row_weight = sb("row_weight", [P, E])
        count = sb("count", [P, E])
        weight = sb("weight", [P, E])
        over = routing([E, TILES], "e r")
        slots_of = sb("slots_of", [P, E])
        before_e = routing([E, E], "e f")
        first_slot = sb("first_slot", [P, E])
        end_slot = sb("end_slot", [P, E])
        slot_expert_f = sb("slot_expert_f", [P, SLOTS])
        slot_expert = sb("slot_expert", [P, SLOTS], I32)
        place = routing([TILES, E], "r e")
        passed = routing([SLOTS, E], "s e")
        pos = sb("pos", [P, PAIRS])
        pos_i = sb("pos_i", [P, 3, PAIRS], I32)
        pos_f = sb("pos_f", [P, 2, PAIRS])
        empty = sb("empty", [P, SLOTS])
        gather_idx = sb("gather_idx", [P, SLOTS], I32)
        scatter_idx = sb("scatter_idx", [P, SLOTS], I32)
        wp1_sb = sb("wp1_sb", [P, KT, PHI])
        bp1_sb = sb("bp1_sb", [P, 1])
        wp2_sb = sb("wp2_sb", [P, 1])
        wp2_bc = sb("wp2_bc", [P, P])
        table_hint = sb("table_hint", [P, 1])
        bp2_bc = sb("bp2_bc", [P, 1])
        mean_w = sb("mean_w", [P, 1])
        pooledT = sb("pooledT", [P, KT, B])
        phi_h = sb("phi_h", [P, B])
        phi = sb("phi", [P, B])
        factor = sb("factor", [P, B])

        ps = stack.enter_context(nc.psum_tensor("ps", [P, 8, 512], F32))
        ctxT_ps = [ps[0:CTX, 3, :], ps[0:CTX, 4, :]]
        wqk_ps = ps[0:CTX, 5, 0:CTX]
        g_ps = [ps[0:CTX, 6, :], ps[0:CTX, 5, :]]
        pair_bank = [7, 0, 1, 2]
        sum_bank = [3, 4, 5, 6]
        logits_ps = ps[:, 3, 0:TILES * E]
        rank_ps = ps[:, 4, 0:TILES * E]
        count_ps = ps[:, 5, 0:E]
        mix_ps = ps[:, 6, 0:E]
        token_ps = ps[:, 7, 0:SLOTS]
        b1T_ps = ps[:, 4, TILES * E:TILES * E + E * HT]
        hT_ps = [ps[:, 2 * n:2 * n + 2, :].rearrange("p a b -> p (a b)")[:, 0:HID]
                 .rearrange("p (c t) -> p c t", c=HT) for n in range(2)]
        zT_ps = ps[:, 4, 0:D].rearrange("p (k t) -> p k t", k=KT)
        y_ps = ps[:, 7, 0:D]
        pool_ps = ps[:, 5, 0:KT * B].rearrange("p (k b) -> p k b", k=KT)
        phi_h_ps = ps[:, 0, 0:B]
        phi_ps = ps[:, 1, 0:B]

        X1_STEPS = 1 + 2 * HALVES + 4

        ctx_loaded = sem("ctx_loaded")
        wqk_loaded = sem("wqk_loaded")
        x_loaded = sem("x_loaded")
        small_loaded = sem("small_loaded")
        weights_loaded = sem("weights_loaded")
        b1_loaded = sem("b1_loaded")
        ones_ready = sem("ones_ready")
        consts_half = sem("consts_half")
        consts = sem("consts")
        ctxT_done = sem("ctxT_done")
        ctxT_copied = sem("ctxT_copied")
        wqk_copied = sem("wqk_copied")
        wqk_done = sem("wqk_done")
        g_done = sem("g_done")
        b1_turned = sem("b1_turned")
        b1_copied = sem("b1_copied")
        rows_hot_pool = sem("rows_hot_pool")
        places_known = sem("places_known")
        g_copied = sem("g_copied")
        sims_done = sem("sims_done")
        sims_copied = sem("sims_copied")
        gates_done = sem("gates_done")
        x_step = sem("x_step")
        base_coefs = sem("base_coefs")
        coef_step = sem("coef_step")
        norm_coefs = sem("norm_coefs")
        var_ready = sem("var_ready")
        root_done = sem("root_done")
        base_done = sem("base_done")
        sig_done = sem("sig_done")
        topk_step = sem("topk_step")
        sims_kept = sem("sims_kept")
        kept_known = sem("kept_known")
        masked = sem("masked")
        last_masked = sem("last_masked")
        last_added = sem("last_added")
        sym_done = sem("sym_done")
        x1_step = sem("x1_step")
        z_done = sem("z_done")
        last_z_done = sem("last_z_done")
        z_stored = sem("z_stored")
        zT_done = sem("zT_done")
        zT_copied = sem("zT_copied")
        logits_done = sem("logits_done")
        route_step = sem("route_step")
        shifted = sem("shifted")
        exp_done = sem("exp_done")
        mix_shifted = sem("mix_shifted")
        mix_exp_done = sem("mix_exp_done")
        chosen_done = sem("chosen_done")
        counts_done = sem("counts_done")
        weights_known = sem("weights_known")
        places_done = sem("places_done")
        tokens_done = sem("tokens_done")
        experts_known = sem("experts_known")
        indices_done = sem("indices_done")
        gathered = [sem("gathered_%d" % n) for n in range(AHEAD)]
        rows_turned = sem("rows_turned")
        rows_copied = sem("rows_copied")
        w1_ready = sem("w1_ready")
        hidden_done = sem("hidden_done")
        y_biased = sem("y_biased")
        hidden_relu = sem("hidden_relu")
        y_done = sem("y_done")
        y_ready = sem("y_ready")
        sum_zeroed = sem("sum_zeroed")
        sum_landed = sem("sum_landed")
        total_loaded = [sem("total_%d_loaded" % b) for b in range(B)]
        wp2_ready = sem("wp2_ready")
        halves_added = sem("halves_added")
        pooled_done = sem("pooled_done")
        pooled_copied = sem("pooled_copied")
        phi_h_done = sem("phi_h_done")
        phi_h_copied = sem("phi_h_copied")
        phi_done = sem("phi_done")
        phi_copied = sem("phi_copied")
        end_step = sem("end_step")
        out_ready = sem("out_ready")
        out_stored = sem("out_stored")
        zeros_ready = sem("zeros_ready")

        block = stack.enter_context(nc.Block())

        @block.sync
        def _(sp):
            sp.dma_start(wqk_sb[:, 0, :], wq).then_inc(wqk_loaded, 16)
            sp.dma_start(wqk_sb[:, 1, :], wk).then_inc(wqk_loaded, 16)
            sp.dma_start(ctx_sb, ctx_rows).then_inc(ctx_loaded, 16)
            sp.dma_start(x_sb[:], x_rows).then_inc(x_loaded, 16)
            for n, g in enumerate((g_xattn, g_ffn, gamma_raw)):
                sp.dma_start(gates[:, n:n + 1], g.rearrange("(a n) -> a n", a=1).to_broadcast([P, 1])
                             ).then_inc(small_loaded, 16)
            sp.dma_start(wr_sb[:], wr.rearrange("(k p) e -> p k e", p=P)).then_inc(small_loaded, 16)
            sp.dma_start(br_bc[:], br.rearrange("(a n) -> a n", a=1).to_broadcast([P, E])
                         ).then_inc(small_loaded, 16)
            sp.dma_start(wp1_sb[:], wp1.rearrange("(k p) j -> p k j", p=P)).then_inc(small_loaded, 16)
            sp.dma_start(bp1_sb[:], bp1.rearrange("(p a) -> p a", a=1)).then_inc(small_loaded, 16)
            sp.dma_start(wp2_sb[:], wp2).then_inc(small_loaded, 16)
            sp.dma_start(bp2_bc[:], bp2.rearrange("(a n) -> a n", a=1).to_broadcast([P, 1])
                         ).then_inc(small_loaded, 16)
            sp.dma_start(b1_rows[:], b1.rearrange("e i -> (e i)").rearrange("(m p) -> m p", p=P)
                         ).then_inc(b1_loaded, 16)
            sp.dma_start(b2_bc[:],
                         b2.rearrange("e d -> (e d)").rearrange("(a n) -> a n", a=1).to_broadcast([P, E * D])
                         ).then_inc(small_loaded, 16)
            for e in range(E):
                sp.dma_start(w1_sb[:, e], w1[e].rearrange("(k p) i -> p k i", p=P)).then_inc(weights_loaded, 16)
                sp.dma_start(w2_sb[:, e], w2[e].rearrange("(c p) d -> p c d", p=P)).then_inc(weights_loaded, 16)
            sp.wait_ge(zeros_ready, 1)
            sp.dma_start(expert_sum.rearrange("(r p) d -> p r d", p=P),
                         zeros[:].rearrange("p (a d) -> p a d", a=1).to_broadcast([P, TILES + 1, D])
                         ).then_inc(sum_zeroed, 16)
            for r in range(TILES):
                if r < TILES - HALVES:
                    sp.wait_ge(z_done, r + 1)
                else:
                    sp.wait_ge(last_z_done, r - (TILES - HALVES) + 1)
                sp.dma_start(normed_rows[r * P:(r + 1) * P, :], z_sb[:, r, :]).then_inc(z_stored, 16)
            sp.wait_ge(sum_landed, 16 * SLOTS)
            for b in range(B):
                sp.dma_start(total_sb[:, b * HALVES:(b + 1) * HALVES, :],
                             expert_sum[b * S:(b + 1) * S, :].rearrange("(r p) d -> p r d", p=P)
                             ).then_inc(total_loaded[b], 16)
            for b in range(B):
                sp.wait_ge(out_ready, b + 1)
                sp.dma_start(out_rows[:, b * HALVES:(b + 1) * HALVES, :],
                             x1_sb[:, b * HALVES:(b + 1) * HALVES, :]).then_inc(out_stored, 16)
            sp.wait_ge(out_stored, 16 * B)

        @block.gpsimd
        def _(pool):
            nc.gpsimd.memset(ones_b[:], 1.0).then_inc(ones_ready, 1)
            nc.gpsimd.memset(ident[:], 0.0)
            nc.gpsimd.memset(zeros[:], 0.0).then_inc(zeros_ready, 1)
            nc.gpsimd.memset(before_b[:], 1.0)
            nc.gpsimd.memset(earlier[:], 1.0)
            nc.gpsimd.memset(mean_w[:], 1.0 / S)
            nc.gpsimd.memset(ones_f[:], 1.0).then_inc(consts_half, 1)
            pool.wait_ge(consts_half, 1)
            nc.gpsimd.affine_select(out=ident[:], in_=ident[:], compare_op=ALU.not_equal, fill=1.0,
                                    base=0, pattern=[[-1, P]], channel_multiplier=1).then_inc(consts, 1)
            nc.gpsimd.affine_select(out=before_b[:], in_=before_b[:], compare_op=ALU.is_gt, fill=0.0,
                                    base=0, pattern=[[1, P]], channel_multiplier=-1)
            nc.gpsimd.affine_select(out=earlier[:], in_=earlier[:], compare_op=ALU.is_gt, fill=0.0,
                                    base=0, pattern=[[1, E], [-1, E]], channel_multiplier=0)
            exact = dict(allow_small_or_imprecise_dtypes=True)
            nc.gpsimd.iota(expert_no[:], pattern=[[1, E]], base=0, channel_multiplier=0, **exact)
            nc.gpsimd.iota(row_no[:], pattern=[[1, P]], base=0, channel_multiplier=0, **exact)
            nc.gpsimd.iota(slot_no_h[:], pattern=[[1, SLOTS]], base=0, channel_multiplier=0, **exact)
            nc.gpsimd.iota(slot_no[:], pattern=[[1, SLOTS]], base=0, channel_multiplier=0, **exact)
            nc.gpsimd.iota(tile_start[:], pattern=[[P, TILES]], base=0, channel_multiplier=0, **exact)
            nc.gpsimd.iota(token_1[:], pattern=[[P, TILES]], base=1, channel_multiplier=1, **exact)
            nc.gpsimd.iota(spare_1[:], pattern=[[0, 1]], base=TOKENS + 1, channel_multiplier=1,
                           **exact).then_inc(consts, 1)

            def gather(s):
                if s >= AHEAD:
                    pool.wait_ge(rows_turned, s - AHEAD + 1)
                nc.gpsimd.indirect_dma_start(
                    out=rows_sb[:, s % AHEAD, :], out_offset=None, in_=normed_rows[:, :],
                    in_offset=bass.IndirectOffsetOnAxis(ap=gather_idx[:, s:s + 1], axis=0),
                ).then_inc(gathered[s % AHEAD], 16)

            for b in range(B - 1):
                pool.wait_ge(sims_kept, b + 1)
                pool.wait_ge(sig_done, b + 1)
                pool.wait_ge(topk_step, (b + 1) * (2 * ROUNDS - 1) * HALVES)
                for r in range(b * HALVES, (b + 1) * HALVES):
                    nc.gpsimd.tensor_scalar(sim_sb[:, r, :], sim_sb[:, r, :], top8[:, r, LAST_COL:LAST_COL + 1], None,
                                            ALU.is_ge).then_inc(kept_known, 1)
                for r in range(b * HALVES, (b + 1) * HALVES):
                    pool.wait_ge(kept_known, r + 1)
                    nc.gpsimd.tensor_mul(a_sb[:, r, :], a_sb[:, r, :], sim_sb[:, r, :]).then_inc(masked, 1)

            pool.wait_ge(places_known, 1)
            for m in range(2 * TILES, PAIRS):
                nc.gpsimd.tensor_scalar(row_hot[:, m, :], row_no[:], pos_f[:, 1, m:m + 1], None, ALU.is_equal
                                        ).then_inc(rows_hot_pool, 1)

            pool.wait_ge(indices_done, 1)
            pool.wait_ge(z_stored, 16 * TILES)
            pool.wait_ge(sum_zeroed, 16)
            for s in range(AHEAD):
                gather(s)
            pool.wait_ge(indices_done, 2)
            for s in range(SLOTS):
                if 1 <= s <= SLOTS - AHEAD:
                    gather(s - 1 + AHEAD)
                pool.wait_ge(y_ready, s + 1)
                if s >= 1:
                    pool.wait_ge(sum_landed, 16 * s)
                nc.gpsimd.indirect_dma_start(
                    out=expert_sum[:, :],
                    out_offset=bass.IndirectOffsetOnAxis(ap=scatter_idx[:, s:s + 1], axis=0),
                    in_=y_sb[:, s % 2, :], in_offset=None, compute_op=ALU.add,
                ).then_inc(sum_landed, 16)

        @block.tensor
        def _(pe):
            def keep_warm(bank, times):
                for _ in range(times):
                    nc.tensor.matmul(ps[:, bank, :], ones_b[:], ones_b[:].rearrange("p (a t) -> p a t", a=1)
                                     .to_broadcast([P, 4, P]), start=True, stop=True)

            pe.wait_ge(ones_ready, 1)
            keep_warm(0, 6)
            pe.wait_ge(wqk_loaded, 32)
            nc.tensor.matmul(wqk_ps, wqk_sb[:, 0, :], wqk_sb[:, 1, :], start=True, stop=True).then_inc(wqk_done, 1)
            keep_warm(0, 3)
            pe.wait_ge(consts, 1)
            pe.wait_ge(ctx_loaded, 16)
            for r in range(TILES):
                turned = nc.tensor.transpose(ctxT_ps[r // 4][:, (r % 4) * P:(r % 4 + 1) * P], ctx_sb[:, r, :],
                                             ident[:])
                if r % 4 == 3:
                    turned.then_inc(ctxT_done, 1)
            pe.wait_ge(wqk_copied, 1)
            for half in range(2):
                pe.wait_ge(ctxT_copied, half + 1)
                nc.tensor.matmul(g_ps[half], wqk_product, cT[:, half * 512:(half + 1) * 512],
                                 start=True, stop=True).then_inc(g_done, 1)
                pe.wait_ge(g_copied, half + 1)
                for b in (2 * half, 2 * half + 1):
                    for i in range(HALVES):
                        r = b * HALVES + i
                        last = nc.tensor.matmul(ps[:, pair_bank[b], i * S:(i + 1) * S], gT[:, r * P:(r + 1) * P],
                                                cT[:, b * S:(b + 1) * S], start=True, stop=True)
                    last.then_inc(sims_done, 1)

            def sum_both(b):
                pe.wait_ge(masked, (b + 1) * HALVES)
                for half in range(HALVES):
                    to = ps[:, sum_bank[b], half * S:(half + 1) * S]
                    nc.tensor.matmul(to, ident[:], a_sb[:, b * HALVES + half, :], start=True, stop=False)
                    for j in range(HALVES):
                        last = nc.tensor.matmul(to[:, j * P:(j + 1) * P],
                                                a_sb[:, b * HALVES + j, half * P:(half + 1) * P], ident[:],
                                                start=False, stop=(j == HALVES - 1))
                last.then_inc(sym_done, 1)

            def turn_masked():
                for half in range(HALVES):
                    pe.wait_ge(last_masked, half + 1)
                    for j in range(HALVES):
                        last = nc.tensor.transpose(
                            ps[:, sum_bank[B - 1], j * S + half * P:j * S + (half + 1) * P],
                            a_sb[:, TILES - HALVES + half, j * P:(j + 1) * P], ident[:])
                last.then_inc(sym_done, 1)

            def route(b):
                for half in range(HALVES):
                    r = b * HALVES + half
                    if b < B - 1:
                        pe.wait_ge(z_done, r + 1)
                    else:
                        pe.wait_ge(last_z_done, half + 1)
                    for k in range(KT):
                        col = half * D + k * P
                        last = nc.tensor.transpose(ps[:, pair_bank[b], col:col + P], z_sb[:, r, k * P:(k + 1) * P],
                                                   ident[:])
                last.then_inc(zT_done, 1)
                pe.wait_ge(zT_copied, b + 1)
                for r in range(b * HALVES, (b + 1) * HALVES):
                    for k in range(KT):
                        last = nc.tensor.matmul(logits_ps[:, r * E:(r + 1) * E], zT_all[:, r, k, :], wr_sb[:, k, :],
                                                start=(k == 0), stop=(k == KT - 1))
                last.then_inc(logits_done, 1)

            sum_both(0)
            pe.wait_ge(small_loaded, 160)
            for b in range(1, B - 1):
                sum_both(b)
                route(b - 1)
            pe.wait_ge(topk_step, ((B - 1) * (2 * ROUNDS - 1) + 12) * HALVES)
            keep_warm(sum_bank[B - 2], 13)
            turn_masked()
            route(B - 2)
            pe.wait_ge(b1_loaded, 16)
            pe.wait_ge(x1_step, X1_STEPS * 2)
            nc.tensor.transpose(b1T_ps, b1_rows[:], ident[0:E * HT, 0:E * HT]).then_inc(b1_turned, 1)
            keep_warm(sum_bank[B - 2], 3)
            route(B - 1)
            pe.wait_ge(chosen_done, 1)
            pe.wait_ge(consts, 2)
            for j in range(TILES):
                last = nc.tensor.matmul(count_ps, ones_b[:], chosen[:, j, :], start=(j == 0), stop=(j == TILES - 1))
            last.then_inc(counts_done, 1)
            chosen_flat = chosen[:].rearrange("p r e -> p (r e)")
            nc.tensor.matmul(rank_ps, before_b[:], chosen_flat, start=True, stop=False)
            for j in range(TILES - 1):
                later = TILES - 1 - j
                last = nc.tensor.matmul(
                    rank_ps[:, (j + 1) * E:].rearrange("p (r e) -> p r e", e=E), ones_b[:],
                    chosen[:, j:j + 1, :].to_broadcast([P, later, E]), start=False, stop=(j == TILES - 2))
            last.then_inc(counts_done, 1)
            for m in range(PAIRS):
                if m < 2 * TILES:
                    pe.wait_ge(places_done, m + 1)
                else:
                    pe.wait_ge(rows_hot_pool, m - 2 * TILES + 1)
                last = nc.tensor.matmul(token_ps, row_hot[:, m, :], slot_token[:, m, :], start=(m == 0),
                                        stop=(m == PAIRS - 1))
            last.then_inc(tokens_done, 1)

            def turn_rows(s, buf, nth):
                pe.wait_ge(gathered[buf], nth * 16 + 16)
                for k in range(KT):
                    last = nc.tensor.transpose(zT_ps[:, k, :], rows_sb[:, buf, k * P:(k + 1) * P], ident[:])
                last.then_inc(rows_turned, 1)

            def first_product(s, odd):
                pe.wait_ge(rows_copied, s + 1)
                pe.wait_ge(w1_ready, s + 1)
                if not isinstance(s, int) or s >= 2:
                    pe.wait_ge(hidden_relu, s - 1)
                for c in range(HT):
                    for k in range(KT):
                        last = nc.tensor.matmul(
                            hT_ps[odd][:, c, :], slot_w1[:, odd, k * HID + c * P:k * HID + (c + 1) * P],
                            zT_sb[:, k, :], start=(k == 0), stop=(k == KT - 1))
                last.then_inc(hidden_done, 1)

            def second_product(s, odd, e):
                pe.wait_ge(hidden_relu, s + 1)
                if not isinstance(s, int) or s >= 1:
                    pe.wait_ge(y_biased, s)
                for c in range(HT):
                    last = nc.tensor.matmul(y_ps, hT_sb[:, odd, c, :], w2_flat[:, bass.ds(e * (HT * D) + c * D, D)],
                                            start=(c == 0), stop=(c == HT - 1))
                last.then_inc(y_done, 1)

            w2_flat = w2_sb[:].rearrange("p e c d -> p (e c d)")

            def expert_of(s):
                return pe.value_load(slot_expert[0:1, bass.ds(s, 1)], min_val=0, max_val=E - 1)

            keep_warm(6, 11)
            turn_rows(0, 0, 0)
            keep_warm(6, 2)
            pe.wait_ge(experts_known, 1)
            pe.wait_ge(weights_loaded, 32 * E)
            first_product(0, 0)
            turn_rows(1, 1, 0)
            pe.wait_ge(chosen_done, 2)
            nc.tensor.matmul(mix_ps, ones_f[:], row_weight[:], start=True, stop=True).then_inc(counts_done, 1)

            def step(s, odd, buf, nth):
                first_product(s, odd)
                turn_rows(s + 1, buf, nth)
                second_product(s - 1, 1 - odd, expert_of(s - 1))

            step(1, 1, 2 % AHEAD, 2 // AHEAD)
            with pe.Fori(0, (SLOTS - 3) // AHEAD) as i:
                for j in range(AHEAD):
                    step(i * AHEAD + 2 + j, j % 2, (3 + j) % AHEAD, i + (3 + j) // AHEAD)
            first_product(SLOTS - 1, 0)
            second_product(SLOTS - 2, 1, expert_of(SLOTS - 2))
            second_product(SLOTS - 1, 0, expert_of(SLOTS - 1))

            keep_warm(6, 28)
            for b in range(B):
                pe.wait_ge(halves_added, b + 1)
                for k in range(KT):
                    last = nc.tensor.matmul(pool_ps[:, k, b:b + 1], both_halves[:, b, k * P:(k + 1) * P], mean_w[:],
                                            start=True, stop=True)
            last.then_inc(pooled_done, 1)
            pe.wait_ge(pooled_copied, 1)
            for k in range(KT):
                last = nc.tensor.matmul(phi_h_ps, wp1_sb[:, k, :], pooledT[:, k, :], start=(k == 0),
                                        stop=(k == KT - 1))
            last.then_inc(phi_h_done, 1)
            pe.wait_ge(phi_h_copied, 1)
            pe.wait_ge(wp2_ready, 1)
            nc.tensor.matmul(phi_ps, wp2_bc[:], phi_h[:], start=True, stop=True).then_inc(phi_done, 1)

        @block.scalar
        def _(act):
            scale = 1.0 / ((CTX // HEADS) ** 0.5 * HEADS)
            act.wait_ge(wqk_done, 1)
            nc.scalar.copy(wqk_product, wqk_ps).then_inc(wqk_copied, 1)
            for half in range(2):
                act.wait_ge(ctxT_done, half + 1)
                nc.scalar.copy(cT[:, half * 512:(half + 1) * 512], ctxT_ps[half]).then_inc(ctxT_copied, 1)
            for half in range(2):
                act.wait_ge(g_done, half + 1)
                nc.scalar.mul(gT[:, half * 512:(half + 1) * 512], g_ps[half], scale).then_inc(g_copied, 1)
                for b in (2 * half, 2 * half + 1):
                    act.wait_ge(sims_done, b + 1)
                    nc.scalar.copy(work_sb[:, b * HALVES:(b + 1) * HALVES, :],
                                   ps[:, pair_bank[b], :].rearrange("p (h s) -> p h s", h=HALVES)
                                   ).then_inc(sims_copied, 1)
            act.wait_ge(small_loaded, 160)
            nc.scalar.activation(gate[:, 0:2], gates[:, 0:2], ACT.Tanh).then_inc(gates_done, 1)
            nc.scalar.activation(gate[:, 2:3], gates[:, 2:3], ACT.Sigmoid).then_inc(gates_done, 1)
            for b in range(B):
                nc.scalar.activation(a_sb[:, b * HALVES:(b + 1) * HALVES, :],
                                     ps[:, pair_bank[b], :].rearrange("p (h s) -> p h s", h=HALVES), ACT.Sigmoid
                                     ).then_inc(sig_done, 1)
                if b < B - 1:
                    nc.scalar.copy(sim_sb[:, b * HALVES:(b + 1) * HALVES, :],
                                   ps[:, pair_bank[b], :].rearrange("p (h s) -> p h s", h=HALVES)
                                   ).then_inc(sims_kept, 1)
            act.wait_ge(consts, 2)
            nc.scalar.activation(wp2_bc[:], ones_f[:], ACT.Copy, scale=wp2_sb[:]).then_inc(wp2_ready, 1)
            act.wait_ge(var_ready, 1)
            nc.scalar.activation(root[:], var_eps[:], ACT.Sqrt).then_inc(root_done, 1)
            act.wait_ge(base_coefs, 1)
            for r in range(TILES):
                nc.scalar.activation(x1_sb[:, r, :], x_sb[:, r, :], ACT.Identity, bias=base_shift[:, r:r + 1],
                                     scale=base_scale[:, r:r + 1]).then_inc(base_done, 1)
            for b in range(B):
                tiles = slice(b * HALVES, (b + 1) * HALVES)
                act.wait_ge(var_ready, b + 2)
                nc.scalar.activation(root[:, tiles], var_eps[:, tiles], ACT.Sqrt).then_inc(root_done, 1)
                if b < B - 1:
                    act.wait_ge(norm_coefs, b + 1)
                for r in range(b * HALVES, min((b + 1) * HALVES, TILES - HALVES)):
                    nc.scalar.activation(z_sb[:, r, :], x1_sb[:, r, :], ACT.Identity, bias=shift[:, r:r + 1],
                                         scale=rstd[:, r:r + 1]).then_inc(z_done, 1)
                act.wait_ge(zT_done, b + 1)
                nc.scalar.copy(zT_all[:, tiles].rearrange("p h k t -> p h (k t)"),
                               ps[:, pair_bank[b], :].rearrange("p (h s) -> p h s", h=HALVES)
                               ).then_inc(zT_copied, 1)
            act.wait_ge(b1_turned, 1)
            nc.scalar.copy(b1T[:], b1T_ps).then_inc(b1_copied, 1)
            act.wait_ge(shifted, 1)
            nc.scalar.activation(probs, logits, ACT.Exp).then_inc(exp_done, 1)
            act.wait_ge(mix_shifted, 1)
            nc.scalar.activation(mix[:], mix[:], ACT.Exp).then_inc(mix_exp_done, 1)
            nc.scalar.activation(table_hint[:], bp2_bc[:], ACT.Sigmoid)

            def copy_rows(s):
                act.wait_ge(rows_turned, s + 1)
                nc.scalar.copy(zT_sb, zT_ps).then_inc(rows_copied, 1)

            def relu_hidden(s, odd, e):
                act.wait_ge(hidden_done, s + 1)
                if not isinstance(s, int) or s >= 2:
                    act.wait_ge(y_done, s - 1)
                for c in range(HT):
                    last = nc.scalar.activation(hT_sb[:, odd, c, :], hT_ps[odd][:, c, :], ACT.Relu,
                                                bias=b1T[:, bass.ds(e * HT + c, 1)])
                last.then_inc(hidden_relu, 1)

            def expert_of(s):
                return act.value_load(slot_expert[0:1, bass.ds(s, 1)], min_val=0, max_val=E - 1)

            copy_rows(0)
            copy_rows(1)
            act.wait_ge(experts_known, 1)
            act.wait_ge(b1_copied, 1)
            relu_hidden(0, 0, expert_of(0))
            copy_rows(2)
            relu_hidden(1, 1, expert_of(1))
            with act.Fori(1, (SLOTS - 1) // 2) as i:
                copy_rows(i * 2 + 1)
                relu_hidden(i * 2, 0, expert_of(i * 2))
                copy_rows(i * 2 + 2)
                relu_hidden(i * 2 + 1, 1, expert_of(i * 2 + 1))
            relu_hidden(SLOTS - 1, 0, expert_of(SLOTS - 1))

            act.wait_ge(phi_h_done, 1)
            nc.scalar.activation(phi_h[:], phi_h_ps, ACT.Relu, bias=bp1_sb[:]).then_inc(phi_h_copied, 1)
            act.wait_ge(phi_done, 1)
            nc.scalar.activation(phi[:], phi_ps, ACT.Sigmoid, bias=bp2_bc[:]).then_inc(phi_copied, 1)

        @block.vector
        def _(dve):
            dve.wait_ge(x_loaded, 16)

            def x_stats(tiles):
                for r in tiles:
                    nc.vector.bn_stats(stats[:, r, :], x_sb[:, r, :]).then_inc(x_step, 1)

            def x_variance():
                for r in range(TILES):
                    dve.wait_ge(x_step, r + 1)
                    nc.vector.bn_aggr(mv[:, r, :], stats[:, r, :]).then_inc(x_step, 1)

            x_stats(range(TILES - 2))

            def invert_root(tiles, nth, step):
                dve.wait_ge(root_done, nth)
                nc.vector.reciprocal(rstd[:, tiles], root[:, tiles]).then_inc(step, 1)

            def newton_1(tiles, step, n):
                dve.wait_ge(step, n + 1)
                nc.vector.scalar_tensor_tensor(out=newton[:, tiles], in0=rstd[:, tiles], scalar=-0.5,
                                               in1=rstd[:, tiles], op0=ALU.mult, op1=ALU.mult).then_inc(step, 1)

            def newton_2(tiles, step, n):
                dve.wait_ge(step, n + 2)
                nc.vector.tensor_mul(newton[:, tiles], newton[:, tiles], var_eps[:, tiles]).then_inc(step, 1)

            def newton_3(tiles, step, n):
                dve.wait_ge(step, n + 3)
                nc.vector.scalar_tensor_tensor(out=rstd[:, tiles], in0=newton[:, tiles], scalar=1.5,
                                               in1=rstd[:, tiles], op0=ALU.add, op1=ALU.mult).then_inc(step, 1)

            def mean_shift(tiles, step, n, signal):
                dve.wait_ge(step, n + 4)
                nc.vector.scalar_tensor_tensor(out=shift[:, tiles], in0=mv[:, tiles, 0], scalar=-1.0,
                                               in1=rstd[:, tiles], op0=ALU.mult, op1=ALU.mult).then_inc(signal, 1)

            def gate_coefs():
                dve.wait_ge(gates_done, 2)
                nc.vector.tensor_mul(coef[:, 0:1], gate[:, 0:1], gate[:, 2:3]).then_inc(coef_step, 1)
                dve.wait_ge(coef_step, 1)
                nc.vector.tensor_sub(coef[:, 1:2], gate[:, 0:1], coef[:, 0:1])
                nc.vector.tensor_scalar_mul(coef[:, 2:3], coef[:, 0:1], 0.5).then_inc(coef_step, 1)

            def base_coefficients():
                dve.wait_ge(x_step, 2 * TILES + 5)
                dve.wait_ge(coef_step, 2)
                nc.vector.tensor_scalar(base_scale[:], rstd[:], coef[:, 1:2], 1.0, ALU.mult, ALU.add)
                nc.vector.tensor_scalar(base_shift[:], shift[:], coef[:, 1:2], None, ALU.mult
                                        ).then_inc(base_coefs, 1)

            def make_x1(b):
                dve.wait_ge(sym_done, b + 1)
                dve.wait_ge(base_done, (b + 1) * HALVES)
                rows = x1_sb[:, b * HALVES:(b + 1) * HALVES, :]
                nc.vector.scalar_tensor_tensor(
                    out=rows, in0=ps[:, sum_bank[b], :].rearrange("p (h s) -> p h s", h=HALVES),
                    scalar=coef[:, 2:3], in1=rows, op0=ALU.mult, op1=ALU.add).then_inc(x1_step, 1)

            def x1_stats(b):
                dve.wait_ge(x1_step, b * X1_STEPS + 1)
                for r in range(b * HALVES, (b + 1) * HALVES):
                    nc.vector.bn_stats(stats[:, r, :], x1_sb[:, r, :]).then_inc(x1_step, 1)

            def x1_variance(b):
                for half in range(HALVES):
                    r = b * HALVES + half
                    dve.wait_ge(x1_step, b * X1_STEPS + 2 + half)
                    nc.vector.bn_aggr(mv[:, r, :], stats[:, r, :]).then_inc(x1_step, 1)

            def x1_variance_eps(b):
                tiles = slice(b * HALVES, (b + 1) * HALVES)
                dve.wait_ge(x1_step, b * X1_STEPS + 1 + 2 * HALVES)
                nc.vector.tensor_scalar_add(var_eps[:, tiles], mv[:, tiles, 1], EPS).then_inc(var_ready, 1)

            every = slice(0, TILES)
            x_n = 2 * TILES
            for b in range(B):
                start = b * HALVES * (2 * ROUNDS - 1)
                at = 5
                before = slice((b - 1) * HALVES, b * HALVES)
                root_n = (b - 1) * X1_STEPS + 1 + 2 * HALVES
                for j in range(ROUNDS):
                    if j > 0:
                        for half in range(HALVES):
                            r = b * HALVES + half
                            dve.wait_ge(topk_step, start + (2 * j - 2) * HALVES + half + 1)
                            nc.vector.match_replace(work_sb[:, r, :], top8[:, r, :], work_sb[:, r, :], LOWEST
                                                    ).then_inc(topk_step, 1)
                        if b >= 1 and j == at + 3:
                            newton_1(before, x1_step, root_n)
                        if b >= 1 and j == at + 4:
                            newton_3(before, x1_step, root_n)
                        if b == 1 and j == 1:
                            newton_1(every, x_step, x_n)
                        if b == 1 and j == 2:
                            newton_3(every, x_step, x_n)
                    for half in range(HALVES):
                        r = b * HALVES + half
                        if j == 0:
                            dve.wait_ge(sims_copied, b + 1)
                        else:
                            dve.wait_ge(topk_step, start + (2 * j - 1) * HALVES + half + 1)
                        nc.vector.max(top8[:, r, :], work_sb[:, r, :]).then_inc(topk_step, 1)
                    if b == 0 and j == 0:
                        x_stats(range(TILES - 2, TILES))
                    if b == 0 and j == 1:
                        x_variance()
                    if b == 0 and j == 2:
                        dve.wait_ge(x_step, 2 * TILES)
                        nc.vector.tensor_scalar_add(var_eps[:], mv[:, :, 1], EPS).then_inc(var_ready, 1)
                    if b == 0 and j == ROUNDS - 1:
                        gate_coefs()
                    if b == 1 and j == 0:
                        invert_root(every, 1, x_step)
                    if b == 1 and j == 1:
                        newton_2(every, x_step, x_n)
                    if b == 1 and j == 2:
                        mean_shift(every, x_step, x_n, x_step)
                    if b == 1 and j == 3:
                        base_coefficients()
                    if b >= 1 and j == at:
                        make_x1(b - 1)
                        x1_stats(b - 1)
                        x1_variance(b - 1)
                    if b >= 1 and j == at + 1:
                        x1_variance_eps(b - 1)
                    if b >= 1 and j == at + 2:
                        invert_root(before, b + 1, x1_step)
                    if b >= 1 and j == at + 3:
                        newton_2(before, x1_step, root_n)
                    if b >= 1 and j == at + 4:
                        mean_shift(before, x1_step, root_n, norm_coefs)
            dve.wait_ge(sig_done, B)
            for half in range(HALVES):
                r = TILES - HALVES + half
                dve.wait_ge(topk_step, (B * (2 * ROUNDS - 1) - 1) * HALVES + half + 1)
                nc.vector.scalar_tensor_tensor(
                    out=a_sb[:, r, :], in0=ps[:, pair_bank[B - 1], half * S:(half + 1) * S],
                    scalar=top8[:, r, LAST_COL:LAST_COL + 1], in1=a_sb[:, r, :],
                    op0=ALU.is_ge, op1=ALU.mult).then_inc(last_masked, 1)
            dve.wait_ge(base_done, TILES)
            dve.wait_ge(last_masked, HALVES)
            rows = x1_sb[:, TILES - HALVES:, :]
            nc.vector.scalar_tensor_tensor(out=rows, in0=a_sb[:, TILES - HALVES:, :], scalar=coef[:, 2:3], in1=rows,
                                           op0=ALU.mult, op1=ALU.add).then_inc(last_added, 1)
            dve.wait_ge(last_added, 1)
            make_x1(B - 1)
            x1_stats(B - 1)
            x1_variance(B - 1)
            x1_variance_eps(B - 1)
            last_tiles = slice((B - 1) * HALVES, TILES)
            root_n = (B - 1) * X1_STEPS + 1 + 2 * HALVES
            invert_root(last_tiles, B + 1, x1_step)
            newton_1(last_tiles, x1_step, root_n)
            newton_2(last_tiles, x1_step, root_n)
            newton_3(last_tiles, x1_step, root_n)
            dve.wait_ge(x1_step, root_n + 4)
            for r in range(TILES - HALVES, TILES):
                nc.vector.tensor_scalar(z_sb[:, r, :], x1_sb[:, r, :], mv[:, r, 0:1], rstd[:, r:r + 1],
                                        ALU.subtract, ALU.mult).then_inc(last_z_done, 1)

            steps = [0]

            def landed(instruction):
                steps[0] += 1
                instruction.then_inc(route_step, 1)
                dve.wait_ge(route_step, steps[0])


            tiles_e = [P, TILES, E]
            dve.wait_ge(consts, 2)
            dve.wait_ge(logits_done, B)
            landed(nc.vector.tensor_add(
                logits, logits_ps.rearrange("p (r e) -> p r e", e=E),
                br_bc[:].rearrange("p (a e) -> p a e", a=1).to_broadcast(tiles_e)))
            landed(nc.vector.reduce_max(row_max[:], logits, AX_X))
            row_all = row_max[:].rearrange("p (r a) -> p r a", a=1).to_broadcast(tiles_e)
            nc.vector.tensor_sub(logits, logits, row_all).then_inc(shifted, 1)
            dve.wait_ge(exp_done, 1)
            landed(nc.vector.reduce_sum(row_max[:], probs, AX_X))
            landed(nc.vector.reciprocal(row_max[:], row_max[:]))
            landed(nc.vector.tensor_mul(probs, probs, row_all))
            for r in range(TILES):
                largest = nc.vector.max(top_p[:, r, :], probs[:, r, :])
            landed(largest)
            for r in range(TILES):
                where = nc.vector.max_index(top_i[:, r, :], top_p[:, r, :], probs[:, r, :])
            tiles_k = [P, TILES, TOP_E]
            nc.vector.tensor_sub(mix[:], top_p[:, :, 0:TOP_E], top_p[:, :, 0:1].to_broadcast(tiles_k)
                                 ).then_inc(mix_shifted, 1)
            landed(where)
            landed(nc.vector.tensor_copy(pick[:], top_i[:, :, 0:TOP_E]))
            hot_shape = [P, TOP_E, TILES, E]
            for k in range(TOP_E):
                made = nc.vector.tensor_tensor(
                    hot[:, k], expert_no[:].rearrange("p (a e) -> p a e", a=1).to_broadcast(tiles_e),
                    pick[:, :, k:k + 1].to_broadcast(tiles_e), ALU.is_equal)
            landed(made)
            with nc.allow_low_precision("sums of at most three zeros and ones"):
                nc.vector.tensor_reduce(chosen[:], hot.rearrange("p k r e -> p r e k"), AX_X, ALU.add
                                        ).then_inc(chosen_done, 1)
            dve.wait_ge(counts_done, 1)
            landed(nc.vector.tensor_tensor(
                over, count_ps.rearrange("p (e a) -> p e a", a=1).to_broadcast([P, E, TILES]),
                tile_start[:].rearrange("p (a r) -> p a r", a=1).to_broadcast([P, E, TILES]), ALU.is_gt))
            landed(nc.vector.reduce_sum(slots_of[:], over, AX_X))
            landed(nc.vector.tensor_mul(before_e, earlier[:], slots_of[:].rearrange("p (a e) -> p a e", a=1)
                                        .to_broadcast([P, E, E])))
            landed(nc.vector.reduce_sum(first_slot[:], before_e, AX_X))
            dve.wait_ge(counts_done, 2)
            landed(nc.vector.scalar_tensor_tensor(
                out=place, in0=first_slot[:].rearrange("p (a e) -> p a e", a=1).to_broadcast(tiles_e),
                scalar=float(P), in1=rank_ps.rearrange("p (r e) -> p r e", e=E), op0=ALU.mult, op1=ALU.add))
            for k in range(TOP_E):
                made = nc.vector.tensor_mul(hot_x[:, k], hot[:, k], place)
            landed(made)
            landed(nc.vector.reduce_sum(pos[:], hot_x.rearrange("p k r e -> p (k r) e"), AX_X))
            landed(nc.vector.tensor_copy(pos_i[:, 0, :], pos[:]))
            nc.vector.tensor_single_scalar(pos_i[:, 1, :], pos_i[:, 0, :], 7, ALU.arith_shift_right)
            landed(nc.vector.tensor_single_scalar(pos_i[:, 2, :], pos_i[:, 0, :], P - 1, ALU.bitwise_and))
            nc.vector.tensor_copy(pos_f[:], pos_i[:, 1:3, :]).then_inc(places_known, 1)
            dve.wait_ge(places_known, 1)
            pair_slots = [P, PAIRS, SLOTS]
            nc.vector.tensor_tensor(
                slot_hot[:], slot_no_h[:].rearrange("p (a s) -> p a s", a=1).to_broadcast(pair_slots),
                pos_f[:, 0, :].rearrange("p (m a) -> p m a", a=1).to_broadcast(pair_slots), ALU.is_equal
            ).then_inc(places_known, 1)
            nc.vector.tensor_scalar(row_hot[:, 0, :], row_no[:], pos_f[:, 1, 0:1], None, ALU.is_equal)
            dve.wait_ge(places_known, 2)
            nc.vector.tensor_tensor(
                slot_token[:].rearrange("p (k r) s -> p k r s", k=TOP_E),
                slot_hot[:].rearrange("p (k r) s -> p k r s", k=TOP_E),
                token_1[:].rearrange("p (a r b) -> p a r b", a=1, b=1).to_broadcast([P, TOP_E, TILES, SLOTS]),
                ALU.mult).then_inc(places_done, 1)
            for m in range(1, 2 * TILES):
                nc.vector.tensor_scalar(row_hot[:, m, :], row_no[:], pos_f[:, 1, m:m + 1], None, ALU.is_equal
                                        ).then_inc(places_done, 1)
            landed(nc.vector.tensor_add(end_slot[:], first_slot[:], slots_of[:]))
            dve.wait_ge(tokens_done, 1)
            nc.vector.tensor_scalar(gather_idx[:], token_ps, -1.0, 0.0, ALU.add, ALU.max).then_inc(indices_done, 1)
            landed(nc.vector.tensor_scalar(empty[:], token_ps, 0.0, spare_1[:], ALU.is_equal, ALU.mult))
            nc.vector.scalar_tensor_tensor(out=scatter_idx[:], in0=token_ps, scalar=-1.0, in1=empty[:],
                                           op0=ALU.add, op1=ALU.add).then_inc(indices_done, 1)
            slot_e = [P, SLOTS, E]
            landed(nc.vector.tensor_tensor(
                passed, slot_no[:].rearrange("p (s a) -> p s a", a=1).to_broadcast(slot_e),
                end_slot[:].rearrange("p (a e) -> p a e", a=1).to_broadcast(slot_e), ALU.is_ge))
            landed(nc.vector.reduce_sum(slot_expert_f[:], passed, AX_X))
            nc.vector.tensor_scalar(slot_expert[:], slot_expert_f[:], float(E - 1), None, ALU.min).then_inc(
                experts_known, 1)

            def expert_of(s):
                return dve.value_load(slot_expert[0:1, bass.ds(s, 1)], min_val=0, max_val=E - 1)

            w1_flat = w1_sb[:].rearrange("p e k i -> p (e k i)")

            def copy_w1(s, odd, e):
                if not isinstance(s, int) or s >= 2:
                    dve.wait_ge(hidden_done, s - 1)
                nc.vector.tensor_copy(slot_w1[:, odd, :], w1_flat[:, bass.ds(e * (KT * HID), KT * HID)]
                                      ).then_inc(w1_ready, 1)

            dve.wait_ge(experts_known, 1)
            dve.wait_ge(weights_loaded, 32 * E)
            copy_w1(0, 0, expert_of(0))
            copy_w1(1, 1, expert_of(1))
            dve.wait_ge(mix_exp_done, 1)
            landed(nc.vector.reduce_sum(row_max[:], mix[:], AX_X))
            landed(nc.vector.reciprocal(row_max[:], row_max[:]))
            landed(nc.vector.tensor_mul(mix[:], mix[:], row_max[:].rearrange("p (r a) -> p r a", a=1)
                                        .to_broadcast(tiles_k)))
            for k in range(TOP_E):
                made = nc.vector.tensor_mul(hot_x[:, k], hot[:, k], mix[:, :, k:k + 1].to_broadcast(tiles_e))
            landed(made)
            nc.vector.tensor_reduce(row_weight[:], hot_x.rearrange("p k r e -> p e (k r)"), AX_X, ALU.add
                                    ).then_inc(chosen_done, 1)
            landed(nc.vector.tensor_scalar(count[:], count_ps, 1.0, None, ALU.max))
            landed(nc.vector.reciprocal(count[:], count[:]))
            dve.wait_ge(counts_done, 3)
            nc.vector.tensor_mul(weight[:], mix_ps, count[:]).then_inc(weights_known, 1)
            dve.wait_ge(weights_known, 1)

            def finish_slot(s, odd, e):
                dve.wait_ge(y_done, s + 1)
                if not isinstance(s, int) or s >= 2:
                    dve.wait_ge(sum_landed, s * 16 - 16)
                nc.vector.tensor_add(y_sb[:, odd, :], y_ps, b2_bc[:, bass.ds(e * D, D)]).then_inc(y_biased, 1)
                dve.wait_ge(y_biased, s + 1)
                nc.vector.tensor_scalar(y_sb[:, odd, :], y_sb[:, odd, :], weight[:, bass.ds(e, 1)], None, ALU.mult
                                        ).then_inc(y_ready, 1)

            copy_w1(2, 0, expert_of(2))
            finish_slot(0, 0, expert_of(0))
            copy_w1(3, 1, expert_of(3))
            finish_slot(1, 1, expert_of(1))
            with dve.Fori(1, (SLOTS - 3) // 2) as i:
                copy_w1(i * 2 + 2, 0, expert_of(i * 2 + 2))
                finish_slot(i * 2, 0, expert_of(i * 2))
                copy_w1(i * 2 + 3, 1, expert_of(i * 2 + 3))
                finish_slot(i * 2 + 1, 1, expert_of(i * 2 + 1))
            copy_w1(SLOTS - 1, 0, expert_of(SLOTS - 1))
            for s in range(SLOTS - 3, SLOTS):
                finish_slot(s, s % 2, expert_of(s))

            for b in range(B):
                dve.wait_ge(total_loaded[b], 16)
                nc.vector.tensor_add(both_halves[:, b, :], total_sb[:, b * HALVES, :], total_sb[:, b * HALVES + 1, :]
                                     ).then_inc(halves_added, 1)
            dve.wait_ge(pooled_done, 1)
            nc.vector.tensor_copy(pooledT[:], pool_ps).then_inc(pooled_copied, 1)
            dve.wait_ge(phi_copied, 1)
            nc.vector.tensor_scalar(factor[:], phi[:], 0.7, -0.8, ALU.is_gt, ALU.mult).then_inc(end_step, 1)
            dve.wait_ge(end_step, 1)
            nc.vector.tensor_scalar(factor[:], factor[:], 1.0, gate[:, 1:2], ALU.add, ALU.mult).then_inc(end_step, 1)
            dve.wait_ge(end_step, 2)
            for b in range(B):
                rows = x1_sb[:, b * HALVES:(b + 1) * HALVES, :]
                nc.vector.scalar_tensor_tensor(
                    out=rows, in0=total_sb[:, b * HALVES:(b + 1) * HALVES, :], scalar=factor[:, b:b + 1],
                    in1=rows, op0=ALU.mult, op1=ALU.add).then_inc(out_ready, 1)


_INS = ["x", "ctx_512", "g_xattn", "g_ffn", "L0_xattn_Wq", "L0_xattn_Wk", "L0_xattn_gamma_raw", "L0_ffn_Wr",
        "L0_ffn_br", "L0_ffn_w1", "L0_ffn_b1", "L0_ffn_w2", "L0_ffn_b2", "L0_ffn_Wp1", "L0_ffn_bp1",
        "L0_ffn_Wp2", "L0_ffn_bp2"]


def kernel(**inputs):
    import numpy as _np
    import concourse.bacc as _bacc
    from concourse import mybir as _mybir
    from concourse.bass_utils import run_bass_kernel_spmd as _run

    nc = _bacc.Bacc("TRN2", target_bir_lowering=False, num_devices=1, dynamic_dma_scratch_size=8192)
    arrays, args = {}, []
    for name in _INS:
        a = _np.ascontiguousarray(inputs[name])
        arrays[f"in_{name}_dram"] = a
        args.append(nc.dram_tensor(f"in_{name}_dram", a.shape, _mybir.dt.from_np(a.dtype), kind="ExternalInput").ap())
    out = nc.dram_tensor("out_0_dram", (B, S, D), _mybir.dt.float32, kind="ExternalOutput").ap()
    flamingo_block(nc, *args, out)
    r = _run(nc, [arrays], core_ids=[0])
    return r.results[0]["out_0_dram"]
```

```python
from contextlib import ExitStack

import concourse.bass as bass
from concourse import mybir

P = 128
F32 = mybir.dt.float32
BF16 = mybir.dt.bfloat16
F16 = mybir.dt.float16
I32 = mybir.dt.int32
U32 = mybir.dt.uint32
ALU = mybir.AluOpType
ACT = mybir.ActivationFunctionType
AX_X = mybir.AxisListType.X

B, S, D = 4, 256, 256
TOKENS = B * S
TILES = TOKENS // P
HALVES = S // P
CTX = 64
HEADS = 4
TOP_ROW = int(S * 0.3)
ROUNDS = (TOP_ROW + 7) // 8
LAST_COL = TOP_ROW - 1 - 8 * (ROUNDS - 1)
E, TOP_E, HID = 12, 3, 640
KT = D // P
HT = HID // P
SLOTS = (TOP_E * TOKENS + E * (P - 1)) // P
EARLY = 6
AHEAD = 4
PHI = D // 2
LOWEST = -3.0e38
EPS = 1e-5


def flamingo_block(nc, x, ctx_in, g_xattn, g_ffn, wq, wk, gamma_raw, wr, br, w1, b1, w2, b2,
                   wp1, bp1, wp2, bp2, out):
    assert HALVES == 2 and SLOTS % 2 == 1 and (SLOTS - 3) % AHEAD == 0 and ROUNDS * 8 - TOP_ROW < 8

    normed_rows = nc.dram_tensor("normed_rows", [TOKENS, D], F32).ap()
    expert_sum = nc.dram_tensor("expert_sum", [TOKENS + P, D], F32).ap()

    x_rows = x.rearrange("b s d -> (b s) d").rearrange("(r p) d -> p r d", p=P)
    ctx_rows = ctx_in.rearrange("b s d -> (b s) d").rearrange("(r p) d -> p r d", p=P)
    out_rows = out.rearrange("b s d -> (b s) d").rearrange("(r p) d -> p r d", p=P)

    with ExitStack() as stack:
        def sb(name, shape, dt=F32):
            return stack.enter_context(nc.sbuf_tensor(name, shape, dt))

        def sem(name):
            return stack.enter_context(nc.semaphore(name))

        w1_sb = sb("w1_sb", [P, E, KT, HID])
        w2_sb = sb("w2_sb", [P, E, HT, D])
        slot_w1 = sb("slot_w1", [P, 2, KT * HID])
        b1_rows = sb("b1_rows", [E * HT, P])
        b1T = sb("b1T", [P, E * HT])
        b2_bc = sb("b2_bc", [P, E * D])
        x_sb = sb("x_sb", [P, TILES, D])
        z_sb = x_sb
        x1_sb = sb("x1_sb", [P, TILES, D])
        zT_all = sb("zT_all", [P, TILES, KT, P])
        work_sb = sb("work_sb", [P, TILES, D])
        a_sb = sb("a_sb", [P, TILES, D])
        flat = sb("shared", [P, 2 * TOKENS + TILES * CTX + 3 * CTX])[:]
        cT = flat[0:CTX, 0:TOKENS]
        gT = flat[0:CTX, TOKENS:2 * TOKENS]
        ctx_sb = flat[:, 2 * TOKENS:2 * TOKENS + TILES * CTX].rearrange("p (r d) -> p r d", r=TILES)
        wqk_sb = flat[0:CTX, 2 * TOKENS + TILES * CTX:][:, 0:2 * CTX].rearrange("p (a d) -> p a d", a=2)
        wqk_product = flat[0:CTX, 2 * TOKENS + TILES * CTX:][:, 2 * CTX:3 * CTX]
        hT_sb = flat[:, 0:2 * HID].rearrange("p (n c t) -> p n c t", n=2, c=HT)
        zT_sb = flat[:, 2 * HID:2 * HID + D].rearrange("p (k t) -> p k t", k=KT)
        y_sb = flat[:, 2 * HID + D:2 * HID + 3 * D].rearrange("p (n d) -> p n d", n=2)
        both_halves = slot_w1[:, 0, 0:B * D].rearrange("p (b d) -> p b d", b=B)
        total_sb = zT_all[:].rearrange("p r k t -> p r (k t)")
        sim_sb = total_sb
        rows_sb = total_sb[:, 0:AHEAD, :]
        PAIRS = TOP_E * TILES
        row_hot = a_sb[:].rearrange("p r d -> p (r d)")[:, 0:PAIRS * P // 2].bitcast(F16).rearrange(
            "p (t m) -> p t m", m=PAIRS)
        slot_hot = sb("slot_hot", [P, SLOTS, PAIRS], F16)
        slot_token = sb("slot_token", [P, SLOTS, PAIRS], F16)
        used = [0]

        def routing(shape, names):
            n = 1
            for size in shape:
                n *= size
            part = work_sb[:].rearrange("p r d -> p (r d)")[:, used[0]:used[0] + n]
            used[0] += n
            assert used[0] <= TILES * D
            sizes = dict(zip(names.split(), shape))
            first = names.split()[:-1]
            return part.rearrange("p (%s) -> p %s" % (names, names), **{a: sizes[a] for a in first})


        ident = sb("ident", [P, P])
        ones_f = sb("ones_f", [P, P])
        ones_b = sb("ones_b", [P, P], BF16)
        before_b = sb("before_b", [P, P], BF16)
        zeros = sb("zeros", [P, D])
        expert_no = sb("expert_no", [P, E])
        row_no = sb("row_no", [P, P, PAIRS], F16)
        slot_no_h = sb("slot_no_h", [P, SLOTS, PAIRS], F16)
        slot_no = sb("slot_no", [P, SLOTS])
        tile_start = sb("tile_start", [P, TILES])
        token_1 = sb("token_1", [P, TOP_E, TILES], F16)
        spare_1 = sb("spare_1", [P, 1])
        earlier = sb("earlier", [P, E, E])

        gates = sb("gates", [P, 3])
        gate = sb("gate", [P, 3])
        coef = sb("coef", [P, 3])
        stats = sb("stats", [P, TILES, 6])
        mv = sb("mv", [P, TILES, 2])
        rstd = sb("rstd", [P, TILES])
        var_eps = sb("var_eps", [P, TILES])
        root = sb("root", [P, TILES])
        newton = sb("newton", [P, TILES])
        row_sum = sb("row_sum", [P, TILES])
        neg_mean = sb("neg_mean", [P, TILES])
        square_sum = sb("square_sum", [P, TILES])
        shift = sb("shift", [P, TILES])
        base_scale = sb("base_scale", [P, TILES])
        base_shift = sb("base_shift", [P, TILES])
        top8 = sb("top8", [P, TILES, 8])
        wr_sb = sb("wr_sb", [P, KT, E])
        br_row = sb("br_row", [1, E])
        logits = routing([TILES, E], "r e")
        row_max = sb("row_max", [P, TILES])
        probs = routing([TILES, E], "r e")
        top_p = sb("top_p", [P, TILES, 8])
        top_i = sb("top_i", [P, TILES, 8], U32)
        mix = sb("mix", [P, TILES, TOP_E])
        hot = routing([TOP_E, TILES, E], "k r e")
        hot_x = routing([TOP_E, TILES, E], "k r e")
        chosen = sb("chosen", [P, TILES, E], BF16)
        row_weight = sb("row_weight", [P, E])
        count = sb("count", [P, E])
        weight = sb("weight", [P, E])
        over = routing([E, TILES], "e r")
        slots_of = sb("slots_of", [P, E])
        before_e = routing([E, E], "e f")
        first_slot = sb("first_slot", [P, E])
        end_slot = sb("end_slot", [P, E])
        slot_expert_f = sb("slot_expert_f", [P, SLOTS])
        slot_expert = sb("slot_expert", [P, SLOTS], I32)
        place = routing([TILES, E], "r e")
        passed = routing([SLOTS, E], "s e")
        pos_i = sb("pos_i", [P, 3, PAIRS], I32)
        pos_h = sb("pos_h", [P, 2, PAIRS], F16)
        empty = sb("empty", [P, SLOTS])
        gather_idx = sb("gather_idx", [P, SLOTS], I32)
        scatter_idx = sb("scatter_idx", [P, SLOTS], I32)
        wp1_sb = sb("wp1_sb", [P, KT, PHI])
        bp1_sb = sb("bp1_sb", [P, 1])
        wp2_sb = sb("wp2_sb", [P, 1])
        wp2_bc = sb("wp2_bc", [P, P])
        table_hint = sb("table_hint", [P, 1])
        bp2_bc = sb("bp2_bc", [P, 1])
        mean_w = sb("mean_w", [P, 1])
        pooledT = sb("pooledT", [P, KT, B])
        phi_h = sb("phi_h", [P, B])
        phi = sb("phi", [P, B])
        factor = sb("factor", [P, B])

        ps = stack.enter_context(nc.psum_tensor("ps", [P, 8, 512], F32))
        ctxT_ps = [ps[0:CTX, 3, :], ps[0:CTX, 4, :]]
        wqk_ps = ps[0:CTX, 5, 0:CTX]
        g_ps = [ps[0:CTX, 6 - b % 2, 0:S] for b in range(B)]
        pair_bank = [7, 0, 1, 2]
        sum_bank = [3, 4, 5, 6]
        logits_ps = ps[:, 3, 0:TILES * E]
        rank_ps = ps[:, 4, 0:TILES * E]
        count_ps = ps[:, 5, 0:E]
        mix_ps = ps[:, 6, 0:E]
        token_ps = ps[:, 7, 0:SLOTS]
        b1T_ps = ps[:, 4, TILES * E:TILES * E + E * HT]
        hT_ps = [ps[:, 2 * n:2 * n + 2, :].rearrange("p a b -> p (a b)")[:, 0:HID]
                 .rearrange("p (c t) -> p c t", c=HT) for n in range(2)]
        zT_ps = ps[:, 4, 0:D].rearrange("p (k t) -> p k t", k=KT)
        y_ps = [ps[:, 7, 0:D], ps[:, 6, 0:D]]
        pool_ps = ps[:, 5, 0:KT * B].rearrange("p (k b) -> p k b", k=KT)
        phi_h_ps = ps[:, 0, 0:B]
        phi_ps = ps[:, 1, 0:B]

        ctx_loaded = sem("ctx_loaded")
        wqk_loaded = sem("wqk_loaded")
        x_loaded = sem("x_loaded")
        small_loaded = sem("small_loaded")
        weights_loaded = sem("weights_loaded")
        b1_loaded = sem("b1_loaded")
        ones_ready = sem("ones_ready")
        consts_half = sem("consts_half")
        consts = sem("consts")
        ctxT_done = sem("ctxT_done")
        ctxT_copied = sem("ctxT_copied")
        wqk_copied = sem("wqk_copied")
        wqk_done = sem("wqk_done")
        g_done = sem("g_done")
        b1_turned = sem("b1_turned")
        b1_copied = sem("b1_copied")
        places_known = sem("places_known")
        g_copied = sem("g_copied")
        sims_done = sem("sims_done")
        sims_copied = sem("sims_copied")
        gates_done = sem("gates_done")
        x_step = sem("x_step")
        base_coefs = sem("base_coefs")
        coef_step = sem("coef_step")
        sum_scaled = sem("sum_scaled")
        rows_added = sem("rows_added")
        rows_summed = sem("rows_summed")
        means_known = sem("means_known")
        squares_summed = sem("squares_summed")
        norm_coefs = sem("norm_coefs")
        var_ready = sem("var_ready")
        root_done = sem("root_done")
        base_done = sem("base_done")
        sig_done = sem("sig_done")
        topk_step = sem("topk_step")
        sims_kept = sem("sims_kept")
        kept_known = sem("kept_known")
        masked = sem("masked")
        last_masked = sem("last_masked")
        last_added = sem("last_added")
        sym_done = sem("sym_done")
        x1_step = sem("x1_step")
        z_done = sem("z_done")
        last_z_done = sem("last_z_done")
        z_stored = sem("z_stored")
        zT_done = sem("zT_done")
        zT_copied = sem("zT_copied")
        logits_done = sem("logits_done")
        route_step = sem("route_step")
        shifted = sem("shifted")
        exp_done = sem("exp_done")
        mix_shifted = sem("mix_shifted")
        mix_exp_done = sem("mix_exp_done")
        chosen_done = sem("chosen_done")
        counts_done = sem("counts_done")
        places_done = sem("places_done")
        tokens_done = sem("tokens_done")
        experts_known = sem("experts_known")
        indices_done = sem("indices_done")
        gathered = [sem("gathered_%d" % n) for n in range(AHEAD)]
        rows_turned = sem("rows_turned")
        rows_copied = sem("rows_copied")
        w1_ready = sem("w1_ready")
        hidden_done = sem("hidden_done")
        y_biased = sem("y_biased")
        hidden_relu = sem("hidden_relu")
        y_done = sem("y_done")
        y_ready = sem("y_ready")
        sum_zeroed = sem("sum_zeroed")
        sum_landed = sem("sum_landed")
        total_loaded = [sem("total_%d_loaded" % b) for b in range(B)]
        wp2_ready = sem("wp2_ready")
        halves_added = sem("halves_added")
        pooled_done = sem("pooled_done")
        pooled_copied = sem("pooled_copied")
        phi_h_done = sem("phi_h_done")
        phi_h_copied = sem("phi_h_copied")
        phi_done = sem("phi_done")
        phi_copied = sem("phi_copied")
        end_step = sem("end_step")
        out_ready = sem("out_ready")
        out_stored = sem("out_stored")
        zeros_ready = sem("zeros_ready")

        block = stack.enter_context(nc.Block())

        @block.sync
        def _(sp):
            sp.dma_start(ctx_sb, ctx_rows).then_inc(ctx_loaded, 16)
            sp.dma_start(wqk_sb[:, 0, :], wq).then_inc(wqk_loaded, 16)
            sp.dma_start(wqk_sb[:, 1, :], wk).then_inc(wqk_loaded, 16)
            sp.dma_start(x_sb[:], x_rows).then_inc(x_loaded, 16)
            for n, g in enumerate((g_xattn, g_ffn, gamma_raw)):
                sp.dma_start(gates[:, n:n + 1], g.rearrange("(a n) -> a n", a=1).to_broadcast([P, 1])
                             ).then_inc(small_loaded, 16)
            sp.dma_start(wr_sb[:], wr.rearrange("(k p) e -> p k e", p=P)).then_inc(small_loaded, 16)
            sp.dma_start(br_row[:], br.rearrange("(a n) -> a n", a=1)).then_inc(small_loaded, 16)
            sp.dma_start(wp1_sb[:], wp1.rearrange("(k p) j -> p k j", p=P)).then_inc(small_loaded, 16)
            sp.dma_start(bp1_sb[:], bp1.rearrange("(p a) -> p a", a=1)).then_inc(small_loaded, 16)
            sp.dma_start(wp2_sb[:], wp2).then_inc(small_loaded, 16)
            sp.dma_start(bp2_bc[:], bp2.rearrange("(a n) -> a n", a=1).to_broadcast([P, 1])
                         ).then_inc(small_loaded, 16)
            sp.dma_start(b1_rows[:], b1.rearrange("e i -> (e i)").rearrange("(m p) -> m p", p=P)
                         ).then_inc(b1_loaded, 16)
            sp.dma_start(b2_bc[:],
                         b2.rearrange("e d -> (e d)").rearrange("(a n) -> a n", a=1).to_broadcast([P, E * D])
                         ).then_inc(small_loaded, 16)
            for e in range(E):
                sp.dma_start(w1_sb[:, e], w1[e].rearrange("(k p) i -> p k i", p=P)).then_inc(weights_loaded, 16)
                sp.dma_start(w2_sb[:, e], w2[e].rearrange("(c p) d -> p c d", p=P)).then_inc(weights_loaded, 16)
            sp.wait_ge(zeros_ready, 1)
            sp.dma_start(expert_sum.rearrange("(r p) d -> p r d", p=P),
                         zeros[:].rearrange("p (a d) -> p a d", a=1).to_broadcast([P, TILES + 1, D])
                         ).then_inc(sum_zeroed, 16)
            for r in range(TILES):
                if r < TILES - HALVES:
                    sp.wait_ge(z_done, r + 1)
                else:
                    sp.wait_ge(last_z_done, r - (TILES - HALVES) + 1)
                sp.dma_start(normed_rows[r * P:(r + 1) * P, :], z_sb[:, r, :]).then_inc(z_stored, 16)
            sp.wait_ge(sum_landed, 16 * SLOTS)
            for b in range(B):
                sp.dma_start(total_sb[:, b * HALVES:(b + 1) * HALVES, :],
                             expert_sum[b * S:(b + 1) * S, :].rearrange("(r p) d -> p r d", p=P)
                             ).then_inc(total_loaded[b], 16)
            for b in range(B):
                sp.wait_ge(out_ready, b + 1)
                sp.dma_start(out_rows[:, b * HALVES:(b + 1) * HALVES, :],
                             x1_sb[:, b * HALVES:(b + 1) * HALVES, :]).then_inc(out_stored, 16)
            sp.wait_ge(out_stored, 16 * B)

        @block.gpsimd
        def _(pool):
            nc.gpsimd.memset(ones_b[:], 1.0).then_inc(ones_ready, 1)
            nc.gpsimd.memset(ident[:], 0.0)
            nc.gpsimd.memset(zeros[:], 0.0).then_inc(zeros_ready, 1)
            nc.gpsimd.memset(before_b[:], 1.0)
            nc.gpsimd.memset(earlier[:], 1.0)
            nc.gpsimd.memset(mean_w[:], 1.0 / S)
            nc.gpsimd.memset(ones_f[:], 1.0).then_inc(consts_half, 1)
            pool.wait_ge(consts_half, 1)
            nc.gpsimd.affine_select(out=ident[:], in_=ident[:], compare_op=ALU.not_equal, fill=1.0,
                                    base=0, pattern=[[-1, P]], channel_multiplier=1).then_inc(consts, 1)
            nc.gpsimd.affine_select(out=before_b[:], in_=before_b[:], compare_op=ALU.is_gt, fill=0.0,
                                    base=0, pattern=[[1, P]], channel_multiplier=-1)
            nc.gpsimd.affine_select(out=earlier[:], in_=earlier[:], compare_op=ALU.is_gt, fill=0.0,
                                    base=0, pattern=[[1, E], [-1, E]], channel_multiplier=0)
            exact = dict(allow_small_or_imprecise_dtypes=True)
            nc.gpsimd.iota(expert_no[:], pattern=[[1, E]], base=0, channel_multiplier=0, **exact)
            nc.gpsimd.iota(row_no[:], pattern=[[1, P], [0, PAIRS]], base=0, channel_multiplier=0, **exact)
            nc.gpsimd.iota(slot_no_h[:], pattern=[[1, SLOTS], [0, PAIRS]], base=0, channel_multiplier=0, **exact)
            nc.gpsimd.iota(slot_no[:], pattern=[[1, SLOTS]], base=0, channel_multiplier=0, **exact)
            nc.gpsimd.iota(tile_start[:], pattern=[[P, TILES]], base=0, channel_multiplier=0, **exact)
            nc.gpsimd.iota(token_1[:], pattern=[[0, TOP_E], [P, TILES]], base=1, channel_multiplier=1, **exact)
            nc.gpsimd.iota(spare_1[:], pattern=[[0, 1]], base=TOKENS + 1, channel_multiplier=1,
                           **exact).then_inc(consts, 1)

            def gather(s):
                if s >= AHEAD:
                    pool.wait_ge(rows_turned, s - AHEAD + 1)
                nc.gpsimd.indirect_dma_start(
                    out=rows_sb[:, s % AHEAD, :], out_offset=None, in_=normed_rows[:, :],
                    in_offset=bass.IndirectOffsetOnAxis(ap=gather_idx[:, s:s + 1], axis=0),
                ).then_inc(gathered[s % AHEAD], 16)

            for b in range(B - 1):
                pool.wait_ge(sims_kept, b + 1)
                pool.wait_ge(sig_done, b + 1)
                pool.wait_ge(topk_step, (b + 1) * (2 * ROUNDS - 1) * HALVES)
                for r in range(b * HALVES, (b + 1) * HALVES):
                    nc.gpsimd.tensor_scalar(sim_sb[:, r, :], sim_sb[:, r, :], top8[:, r, LAST_COL:LAST_COL + 1], None,
                                            ALU.is_ge).then_inc(kept_known, 1)
                for r in range(b * HALVES, (b + 1) * HALVES):
                    pool.wait_ge(kept_known, r + 1)
                    nc.gpsimd.tensor_mul(a_sb[:, r, :], a_sb[:, r, :], sim_sb[:, r, :]).then_inc(masked, 1)
                pool.wait_ge(sum_scaled, b + 1)
                pool.wait_ge(base_done, (b + 1) * HALVES)
                for r in range(b * HALVES, (b + 1) * HALVES):
                    nc.gpsimd.tensor_add(x1_sb[:, r, :], x1_sb[:, r, :], work_sb[:, r, :]).then_inc(rows_added, 1)

            pool.wait_ge(indices_done, 1)
            pool.wait_ge(z_stored, 16 * TILES)
            pool.wait_ge(sum_zeroed, 16)
            for s in range(AHEAD):
                gather(s)
            pool.wait_ge(indices_done, 2)
            for s in range(SLOTS):
                if 1 <= s <= SLOTS - AHEAD:
                    gather(s - 1 + AHEAD)
                pool.wait_ge(y_ready, s + 1)
                if s >= 1:
                    pool.wait_ge(sum_landed, 16 * s)
                nc.gpsimd.indirect_dma_start(
                    out=expert_sum[:, :],
                    out_offset=bass.IndirectOffsetOnAxis(ap=scatter_idx[:, s:s + 1], axis=0),
                    in_=y_sb[:, s % 2, :], in_offset=None, compute_op=ALU.add,
                ).then_inc(sum_landed, 16)

        @block.tensor
        def _(pe):
            def keep_warm(bank, times):
                for _ in range(times):
                    nc.tensor.matmul(ps[:, bank, :], ones_b[:], ones_b[:].rearrange("p (a t) -> p a t", a=1)
                                     .to_broadcast([P, 4, P]), start=True, stop=True)

            pe.wait_ge(ones_ready, 1)
            keep_warm(0, 7)
            pe.wait_ge(consts, 1)
            pe.wait_ge(ctx_loaded, 16)
            for r in range(TILES):
                if r == TILES // 2:
                    pe.wait_ge(wqk_loaded, 32)
                    nc.tensor.matmul(wqk_ps, wqk_sb[:, 0, :], wqk_sb[:, 1, :], start=True, stop=True
                                     ).then_inc(wqk_done, 1)
                turned = nc.tensor.transpose(ctxT_ps[r // 4][:, (r % 4) * P:(r % 4 + 1) * P], ctx_sb[:, r, :],
                                             ident[:])
                if r % 4 == 3:
                    turned.then_inc(ctxT_done, 1)

            def project(b):
                pe.wait_ge(ctxT_copied, b // 2 + 1)
                nc.tensor.matmul(g_ps[b], wqk_product, cT[:, b * S:(b + 1) * S], start=True, stop=True
                                 ).then_inc(g_done, 1)

            pe.wait_ge(wqk_copied, 1)
            project(0)
            for b in range(B):
                if b + 1 < B:
                    project(b + 1)
                pe.wait_ge(g_copied, b + 1)
                for i in range(HALVES):
                    r = b * HALVES + i
                    last = nc.tensor.matmul(ps[:, pair_bank[b], i * S:(i + 1) * S], gT[:, r * P:(r + 1) * P],
                                            cT[:, b * S:(b + 1) * S], start=True, stop=True)
                last.then_inc(sims_done, 1)

            def sum_both(b):
                pe.wait_ge(masked, (b + 1) * HALVES)
                for half in range(HALVES):
                    to = ps[:, sum_bank[b], half * S:(half + 1) * S]
                    nc.tensor.matmul(to, ident[:], a_sb[:, b * HALVES + half, :], start=True, stop=False)
                    for j in range(HALVES):
                        last = nc.tensor.matmul(to[:, j * P:(j + 1) * P],
                                                a_sb[:, b * HALVES + j, half * P:(half + 1) * P], ident[:],
                                                start=False, stop=(j == HALVES - 1))
                last.then_inc(sym_done, 1)

            def turn_masked():
                for half in range(HALVES):
                    pe.wait_ge(last_masked, half + 1)
                    for j in range(HALVES):
                        last = nc.tensor.transpose(
                            ps[:, sum_bank[B - 1], j * S + half * P:j * S + (half + 1) * P],
                            a_sb[:, TILES - HALVES + half, j * P:(j + 1) * P], ident[:])
                last.then_inc(sym_done, 1)

            def route(b):
                for half in range(HALVES):
                    r = b * HALVES + half
                    if b < B - 1:
                        pe.wait_ge(z_done, r + 1)
                    else:
                        pe.wait_ge(last_z_done, half + 1)
                    for k in range(KT):
                        col = half * D + k * P
                        last = nc.tensor.transpose(ps[:, pair_bank[b], col:col + P], z_sb[:, r, k * P:(k + 1) * P],
                                                   ident[:])
                last.then_inc(zT_done, 1)
                if b == 0:
                    nc.tensor.matmul(logits_ps.rearrange("p (r e) -> p r e", e=E), ones_f[0:1, :],
                                     br_row[:].rearrange("p (a e) -> p a e", a=1).to_broadcast([1, TILES, E]),
                                     start=True, stop=False)
                if b >= B - 2:
                    keep_warm(sum_bank[B - 2], 3)
                pe.wait_ge(zT_copied, b + 1)
                for r in range(b * HALVES, (b + 1) * HALVES):
                    for k in range(KT):
                        last = nc.tensor.matmul(logits_ps[:, r * E:(r + 1) * E], zT_all[:, r, k, :], wr_sb[:, k, :],
                                                start=False, stop=(r == TILES - 1 and k == KT - 1))
                last.then_inc(logits_done, 1)

            sum_both(0)
            pe.wait_ge(small_loaded, 160)
            for b in range(1, B - 1):
                sum_both(b)
                route(b - 1)
            pe.wait_ge(sum_scaled, B - 1)
            pe.wait_ge(topk_step, ((B - 1) * (2 * ROUNDS - 1) + 13) * HALVES)
            keep_warm(sum_bank[B - 2], 11)
            turn_masked()
            keep_warm(sum_bank[B - 2], 7)
            route(B - 2)
            pe.wait_ge(b1_loaded, 16)
            pe.wait_ge(sum_scaled, 2)
            nc.tensor.transpose(b1T_ps, b1_rows[:], ident[0:E * HT, 0:E * HT]).then_inc(b1_turned, 1)
            keep_warm(sum_bank[B - 2], 2)
            route(B - 1)
            pe.wait_ge(chosen_done, 1)
            pe.wait_ge(consts, 2)
            for j in range(TILES):
                last = nc.tensor.matmul(count_ps, ones_b[:], chosen[:, j, :], start=(j == 0), stop=(j == TILES - 1))
            last.then_inc(counts_done, 1)
            chosen_flat = chosen[:].rearrange("p r e -> p (r e)")
            nc.tensor.matmul(rank_ps, before_b[:], chosen_flat, start=True, stop=False)
            for j in range(TILES - 1):
                later = TILES - 1 - j
                last = nc.tensor.matmul(
                    rank_ps[:, (j + 1) * E:].rearrange("p (r e) -> p r e", e=E), ones_b[:],
                    chosen[:, j:j + 1, :].to_broadcast([P, later, E]), start=False, stop=(j == TILES - 2))
            last.then_inc(counts_done, 1)
            pe.wait_ge(places_done, 1)
            for m in range(PAIRS):
                last = nc.tensor.matmul(token_ps, row_hot[:, :, m], slot_token[:, :, m], start=(m == 0),
                                        stop=(m == PAIRS - 1))
            last.then_inc(tokens_done, 1)

            def turn_rows(s, buf, nth):
                pe.wait_ge(gathered[buf], nth * 16 + 16)
                for k in range(KT):
                    last = nc.tensor.transpose(zT_ps[:, k, :], rows_sb[:, buf, k * P:(k + 1) * P], ident[:])
                last.then_inc(rows_turned, 1)

            def first_product(s, odd):
                pe.wait_ge(rows_copied, s + 1)
                pe.wait_ge(w1_ready, s + 1)
                if not isinstance(s, int) or s >= 2:
                    pe.wait_ge(hidden_relu, s - 1)
                for c in range(HT):
                    for k in range(KT):
                        last = nc.tensor.matmul(
                            hT_ps[odd][:, c, :], slot_w1[:, odd, k * HID + c * P:k * HID + (c + 1) * P],
                            zT_sb[:, k, :], start=(k == 0), stop=(k == KT - 1))
                last.then_inc(hidden_done, 1)

            def second_product(s, odd, e):
                pe.wait_ge(hidden_relu, s + 1)
                if not isinstance(s, int) or s >= 1:
                    pe.wait_ge(y_biased, s)
                for c in range(HT):
                    last = nc.tensor.matmul(y_ps[odd], hT_sb[:, odd, c, :], w2_flat[:, bass.ds(e * (HT * D) + c * D, D)],
                                            start=(c == 0), stop=(c == HT - 1))
                last.then_inc(y_done, 1)

            w2_flat = w2_sb[:].rearrange("p e c d -> p (e c d)")

            def expert_of(s):
                return pe.value_load(slot_expert[0:1, bass.ds(s, 1)], min_val=0, max_val=E - 1)

            keep_warm(6, 8)
            pe.wait_ge(experts_known, 1)
            pe.wait_ge(weights_loaded, 32 * E)
            turn_rows(0, 0, 0)
            keep_warm(6, 1)
            first_product(0, 0)
            turn_rows(1, 1, 0)
            pe.wait_ge(chosen_done, 2)
            nc.tensor.matmul(mix_ps, ones_f[:], row_weight[:], start=True, stop=True).then_inc(counts_done, 1)

            def step(s, odd, buf, nth):
                first_product(s, odd)
                turn_rows(s + 1, buf, nth)
                second_product(s - 1, 1 - odd, expert_of(s - 1))

            step(1, 1, 2 % AHEAD, 2 // AHEAD)
            with pe.Fori(0, (SLOTS - 3) // AHEAD) as i:
                for j in range(AHEAD):
                    step(i * AHEAD + 2 + j, j % 2, (3 + j) % AHEAD, i + (3 + j) // AHEAD)
            first_product(SLOTS - 1, 0)
            second_product(SLOTS - 2, 1, expert_of(SLOTS - 2))
            second_product(SLOTS - 1, 0, expert_of(SLOTS - 1))

            keep_warm(2, 37)
            for b in range(B):
                if b >= 1:
                    keep_warm(2, 1)
                pe.wait_ge(halves_added, b + 1)
                for k in range(KT):
                    last = nc.tensor.matmul(pool_ps[:, k, b:b + 1], both_halves[:, b, k * P:(k + 1) * P], mean_w[:],
                                            start=True, stop=True)
            last.then_inc(pooled_done, 1)
            keep_warm(2, 1)
            pe.wait_ge(pooled_copied, 1)
            for k in range(KT):
                last = nc.tensor.matmul(phi_h_ps, wp1_sb[:, k, :], pooledT[:, k, :], start=(k == 0),
                                        stop=(k == KT - 1))
            last.then_inc(phi_h_done, 1)
            keep_warm(2, 2)
            pe.wait_ge(phi_h_copied, 1)
            pe.wait_ge(wp2_ready, 1)
            nc.tensor.matmul(phi_ps, wp2_bc[:], phi_h[:], start=True, stop=True).then_inc(phi_done, 1)

        @block.scalar
        def _(act):
            scale = 1.0 / ((CTX // HEADS) ** 0.5 * HEADS)
            for half in range(2):
                act.wait_ge(ctxT_done, half + 1)
                nc.scalar.copy(cT[:, half * 512:(half + 1) * 512], ctxT_ps[half]).then_inc(ctxT_copied, 1)
                if half == 0:
                    act.wait_ge(wqk_done, 1)
                    nc.scalar.copy(wqk_product, wqk_ps).then_inc(wqk_copied, 1)

            def scale_projection(b):
                act.wait_ge(g_done, b + 1)
                nc.scalar.mul(gT[:, b * S:(b + 1) * S], g_ps[b], scale).then_inc(g_copied, 1)

            scale_projection(0)
            for b in range(B):
                if b + 1 < B:
                    scale_projection(b + 1)
                act.wait_ge(sims_done, b + 1)
                nc.scalar.copy(work_sb[:, b * HALVES:(b + 1) * HALVES, :],
                               ps[:, pair_bank[b], :].rearrange("p (h s) -> p h s", h=HALVES)
                               ).then_inc(sims_copied, 1)
            act.wait_ge(small_loaded, 160)
            nc.scalar.activation(gate[:, 0:2], gates[:, 0:2], ACT.Tanh).then_inc(gates_done, 1)
            nc.scalar.activation(gate[:, 2:3], gates[:, 2:3], ACT.Sigmoid).then_inc(gates_done, 1)
            for b in range(B):
                nc.scalar.activation(a_sb[:, b * HALVES:(b + 1) * HALVES, :],
                                     ps[:, pair_bank[b], :].rearrange("p (h s) -> p h s", h=HALVES), ACT.Sigmoid
                                     ).then_inc(sig_done, 1)
                if b < B - 1:
                    nc.scalar.copy(sim_sb[:, b * HALVES:(b + 1) * HALVES, :],
                                   ps[:, pair_bank[b], :].rearrange("p (h s) -> p h s", h=HALVES)
                                   ).then_inc(sims_kept, 1)
            act.wait_ge(consts, 2)
            nc.scalar.activation(wp2_bc[:], ones_f[:], ACT.Copy, scale=wp2_sb[:]).then_inc(wp2_ready, 1)
            act.wait_ge(var_ready, 1)
            nc.scalar.activation(root[:], var_eps[:], ACT.Sqrt).then_inc(root_done, 1)
            act.wait_ge(base_coefs, 1)
            for r in range(TILES):
                nc.scalar.activation(x1_sb[:, r, :], x_sb[:, r, :], ACT.Identity, bias=base_shift[:, r:r + 1],
                                     scale=base_scale[:, r:r + 1]).then_inc(base_done, 1)
            act.wait_ge(coef_step, 2)
            for b in range(B):
                tiles = slice(b * HALVES, (b + 1) * HALVES)
                if b < B - 1:
                    act.wait_ge(sym_done, b + 1)
                    nc.scalar.activation(work_sb[:, tiles, :],
                                         ps[:, sum_bank[b], :].rearrange("p (h s) -> p h s", h=HALVES), ACT.Copy,
                                         scale=coef[:, 2:3]).then_inc(sum_scaled, 1)
                    for r in range(b * HALVES, (b + 1) * HALVES):
                        act.wait_ge(rows_added, r + 1)
                        nc.scalar.activation(work_sb[:, r, :], x1_sb[:, r, :], ACT.Identity,
                                             accum_out=row_sum[:, r:r + 1]).then_inc(rows_summed, 1)
                    act.wait_ge(rows_summed, (b + 1) * HALVES)
                    nc.scalar.mul(neg_mean[:, tiles], row_sum[:, tiles], -1.0 / D).then_inc(means_known, 1)
                    act.wait_ge(means_known, b + 1)
                    for r in range(b * HALVES, (b + 1) * HALVES):
                        nc.scalar.activation(work_sb[:, r, :], x1_sb[:, r, :], ACT.Square, bias=neg_mean[:, r:r + 1],
                                             accum_out=square_sum[:, r:r + 1]).then_inc(squares_summed, 1)
                act.wait_ge(var_ready, b + 2)
                nc.scalar.activation(root[:, tiles], var_eps[:, tiles], ACT.Sqrt).then_inc(root_done, 1)
                if b < B - 1:
                    act.wait_ge(norm_coefs, b + 1)
                for r in range(b * HALVES, min((b + 1) * HALVES, TILES - HALVES)):
                    nc.scalar.activation(z_sb[:, r, :], x1_sb[:, r, :], ACT.Identity, bias=shift[:, r:r + 1],
                                         scale=rstd[:, r:r + 1]).then_inc(z_done, 1)
                act.wait_ge(zT_done, b + 1)
                nc.scalar.copy(zT_all[:, tiles].rearrange("p h k t -> p h (k t)"),
                               ps[:, pair_bank[b], :].rearrange("p (h s) -> p h s", h=HALVES)
                               ).then_inc(zT_copied, 1)
            act.wait_ge(b1_turned, 1)
            nc.scalar.copy(b1T[:], b1T_ps).then_inc(b1_copied, 1)
            act.wait_ge(shifted, 1)
            nc.scalar.activation(probs, logits, ACT.Exp).then_inc(exp_done, 1)
            act.wait_ge(mix_shifted, 1)
            nc.scalar.activation(mix[:], mix[:], ACT.Exp).then_inc(mix_exp_done, 1)
            nc.scalar.activation(table_hint[:], bp2_bc[:], ACT.Sigmoid)

            def copy_rows(s):
                act.wait_ge(rows_turned, s + 1)
                nc.scalar.copy(zT_sb, zT_ps).then_inc(rows_copied, 1)

            def relu_hidden(s, odd, e):
                act.wait_ge(hidden_done, s + 1)
                if not isinstance(s, int) or s >= 2:
                    act.wait_ge(y_done, s - 1)
                for c in range(HT):
                    last = nc.scalar.activation(hT_sb[:, odd, c, :], hT_ps[odd][:, c, :], ACT.Relu,
                                                bias=b1T[:, bass.ds(e * HT + c, 1)])
                last.then_inc(hidden_relu, 1)

            def expert_of(s):
                return act.value_load(slot_expert[0:1, bass.ds(s, 1)], min_val=0, max_val=E - 1)

            copy_rows(0)
            copy_rows(1)
            act.wait_ge(experts_known, 1)
            act.wait_ge(b1_copied, 1)
            relu_hidden(0, 0, expert_of(0))
            copy_rows(2)
            relu_hidden(1, 1, expert_of(1))
            with act.Fori(1, (SLOTS - 1) // 2) as i:
                copy_rows(i * 2 + 1)
                relu_hidden(i * 2, 0, expert_of(i * 2))
                copy_rows(i * 2 + 2)
                relu_hidden(i * 2 + 1, 1, expert_of(i * 2 + 1))
            relu_hidden(SLOTS - 1, 0, expert_of(SLOTS - 1))

            act.wait_ge(phi_h_done, 1)
            nc.scalar.activation(phi_h[:], phi_h_ps, ACT.Relu, bias=bp1_sb[:]).then_inc(phi_h_copied, 1)
            act.wait_ge(phi_done, 1)
            nc.scalar.activation(phi[:], phi_ps, ACT.Sigmoid, bias=bp2_bc[:]).then_inc(phi_copied, 1)

        @block.vector
        def _(dve):
            dve.wait_ge(x_loaded, 16)

            def x_stats(tiles):
                for r in tiles:
                    nc.vector.bn_stats(stats[:, r, :], x_sb[:, r, :]).then_inc(x_step, 1)

            def x_variance():
                for r in range(TILES):
                    dve.wait_ge(x_step, r + 1)
                    nc.vector.bn_aggr(mv[:, r, :], stats[:, r, :]).then_inc(x_step, 1)

            x_stats(range(EARLY))

            def invert_root(tiles, nth, step):
                dve.wait_ge(root_done, nth)
                nc.vector.reciprocal(rstd[:, tiles], root[:, tiles]).then_inc(step, 1)

            def newton_1(tiles, step, n):
                dve.wait_ge(step, n + 1)
                nc.vector.scalar_tensor_tensor(out=newton[:, tiles], in0=rstd[:, tiles], scalar=-0.5,
                                               in1=rstd[:, tiles], op0=ALU.mult, op1=ALU.mult).then_inc(step, 1)

            def newton_2(tiles, step, n):
                dve.wait_ge(step, n + 2)
                nc.vector.tensor_mul(newton[:, tiles], newton[:, tiles], var_eps[:, tiles]).then_inc(step, 1)

            def newton_3(tiles, step, n):
                dve.wait_ge(step, n + 3)
                nc.vector.scalar_tensor_tensor(out=rstd[:, tiles], in0=newton[:, tiles], scalar=1.5,
                                               in1=rstd[:, tiles], op0=ALU.add, op1=ALU.mult).then_inc(step, 1)

            def mean_shift(tiles, step, n, signal):
                dve.wait_ge(step, n + 4)
                nc.vector.scalar_tensor_tensor(out=shift[:, tiles], in0=mv[:, tiles, 0], scalar=-1.0,
                                               in1=rstd[:, tiles], op0=ALU.mult, op1=ALU.mult).then_inc(signal, 1)

            def gate_coefs():
                dve.wait_ge(gates_done, 2)
                nc.vector.tensor_mul(coef[:, 0:1], gate[:, 0:1], gate[:, 2:3]).then_inc(coef_step, 1)
                dve.wait_ge(coef_step, 1)
                nc.vector.tensor_sub(coef[:, 1:2], gate[:, 0:1], coef[:, 0:1])
                nc.vector.tensor_scalar_mul(coef[:, 2:3], coef[:, 0:1], 0.5).then_inc(coef_step, 1)

            def base_coefficients():
                dve.wait_ge(x_step, 2 * TILES + 5)
                dve.wait_ge(coef_step, 2)
                nc.vector.tensor_scalar(base_scale[:], rstd[:], coef[:, 1:2], 1.0, ALU.mult, ALU.add)
                nc.vector.tensor_scalar(base_shift[:], shift[:], coef[:, 1:2], None, ALU.mult
                                        ).then_inc(base_coefs, 1)

            def square_variance(b):
                tiles = slice(b * HALVES, (b + 1) * HALVES)
                dve.wait_ge(squares_summed, (b + 1) * HALVES)
                nc.vector.tensor_scalar(var_eps[:, tiles], square_sum[:, tiles], 1.0 / D, EPS, ALU.mult, ALU.add
                                        ).then_inc(var_ready, 1)

            def square_shift(b):
                tiles = slice(b * HALVES, (b + 1) * HALVES)
                dve.wait_ge(x1_step, b * 4 + 4)
                nc.vector.tensor_mul(shift[:, tiles], neg_mean[:, tiles], rstd[:, tiles]).then_inc(norm_coefs, 1)

            every = slice(0, TILES)
            x_n = 2 * TILES
            for b in range(B):
                start = b * HALVES * (2 * ROUNDS - 1)
                behind = b - 2
                behind_tiles = slice(behind * HALVES, (behind + 1) * HALVES)
                for j in range(ROUNDS):
                    if j > 0:
                        for half in range(HALVES):
                            r = b * HALVES + half
                            dve.wait_ge(topk_step, start + (2 * j - 2) * HALVES + half + 1)
                            nc.vector.match_replace(work_sb[:, r, :], top8[:, r, :], work_sb[:, r, :], LOWEST
                                                    ).then_inc(topk_step, 1)
                        if b >= 2 and j == 1:
                            newton_1(behind_tiles, x1_step, behind * 4)
                        if b >= 2 and j == 2:
                            newton_3(behind_tiles, x1_step, behind * 4)
                        if b == 1 and j == 1:
                            newton_1(every, x_step, x_n)
                        if b == 1 and j == 2:
                            newton_3(every, x_step, x_n)
                    for half in range(HALVES):
                        r = b * HALVES + half
                        if j == 0:
                            dve.wait_ge(sims_copied, b + 1)
                        else:
                            dve.wait_ge(topk_step, start + (2 * j - 1) * HALVES + half + 1)
                        nc.vector.max(top8[:, r, :], work_sb[:, r, :]).then_inc(topk_step, 1)
                    if b == 0 and j == 0:
                        x_stats(range(EARLY, TILES))
                    if b == 0 and j == 1:
                        x_variance()
                    if b == 0 and j == 2:
                        dve.wait_ge(x_step, 2 * TILES)
                        nc.vector.tensor_scalar_add(var_eps[:], mv[:, :, 1], EPS).then_inc(var_ready, 1)
                    if b == 0 and j == ROUNDS - 1:
                        gate_coefs()
                    if b == 1 and j == 0:
                        invert_root(every, 1, x_step)
                    if b == 1 and j == 1:
                        newton_2(every, x_step, x_n)
                    if b == 1 and j == 2:
                        mean_shift(every, x_step, x_n, x_step)
                    if b == 1 and j == 3:
                        base_coefficients()
                    if b >= 1 and j == ROUNDS - 1:
                        square_variance(b - 1)
                    if b >= 2 and j == 0:
                        invert_root(behind_tiles, behind + 2, x1_step)
                    if b >= 2 and j == 1:
                        newton_2(behind_tiles, x1_step, behind * 4)
                    if b >= 2 and j == 2:
                        square_shift(behind)
            dve.wait_ge(sig_done, B)
            for half in range(HALVES):
                r = TILES - HALVES + half
                dve.wait_ge(topk_step, (B * (2 * ROUNDS - 1) - 1) * HALVES + half + 1)
                nc.vector.scalar_tensor_tensor(
                    out=a_sb[:, r, :], in0=ps[:, pair_bank[B - 1], half * S:(half + 1) * S],
                    scalar=top8[:, r, LAST_COL:LAST_COL + 1], in1=a_sb[:, r, :],
                    op0=ALU.is_ge, op1=ALU.mult).then_inc(last_masked, 1)
            near_tiles = slice((B - 2) * HALVES, (B - 1) * HALVES)
            near_n = (B - 2) * 4
            invert_root(near_tiles, B, x1_step)
            dve.wait_ge(base_done, TILES)
            dve.wait_ge(last_masked, HALVES)
            rows = x1_sb[:, TILES - HALVES:, :]
            nc.vector.scalar_tensor_tensor(out=rows, in0=a_sb[:, TILES - HALVES:, :], scalar=coef[:, 2:3], in1=rows,
                                           op0=ALU.mult, op1=ALU.add).then_inc(last_added, 1)
            newton_1(near_tiles, x1_step, near_n)
            newton_2(near_tiles, x1_step, near_n)
            newton_3(near_tiles, x1_step, near_n)
            square_shift(B - 2)
            last_n = (B - 1) * 4
            dve.wait_ge(last_added, 1)
            dve.wait_ge(sym_done, B)
            nc.vector.scalar_tensor_tensor(
                out=rows, in0=ps[:, sum_bank[B - 1], :].rearrange("p (h s) -> p h s", h=HALVES),
                scalar=coef[:, 2:3], in1=rows, op0=ALU.mult, op1=ALU.add).then_inc(x1_step, 1)
            dve.wait_ge(x1_step, last_n + 1)
            for r in range(TILES - HALVES, TILES):
                nc.vector.bn_stats(stats[:, r, :], x1_sb[:, r, :]).then_inc(x1_step, 1)
            for half in range(HALVES):
                r = TILES - HALVES + half
                dve.wait_ge(x1_step, last_n + 2 + half)
                nc.vector.bn_aggr(mv[:, r, :], stats[:, r, :]).then_inc(x1_step, 1)
            last_tiles = slice(TILES - HALVES, TILES)
            root_n = last_n + 1 + 2 * HALVES
            dve.wait_ge(x1_step, root_n)
            nc.vector.tensor_scalar_add(var_eps[:, last_tiles], mv[:, last_tiles, 1], EPS).then_inc(var_ready, 1)
            invert_root(last_tiles, B + 1, x1_step)
            newton_1(last_tiles, x1_step, root_n)
            newton_2(last_tiles, x1_step, root_n)
            newton_3(last_tiles, x1_step, root_n)
            dve.wait_ge(x1_step, root_n + 4)
            for r in range(TILES - HALVES, TILES):
                nc.vector.tensor_scalar(z_sb[:, r, :], x1_sb[:, r, :], mv[:, r, 0:1], rstd[:, r:r + 1],
                                        ALU.subtract, ALU.mult).then_inc(last_z_done, 1)

            steps = [0]

            def landed(instruction):
                steps[0] += 1
                instruction.then_inc(route_step, 1)
                dve.wait_ge(route_step, steps[0])


            tiles_e = [P, TILES, E]
            dve.wait_ge(consts, 2)
            dve.wait_ge(logits_done, B)
            raw_logits = logits_ps.rearrange("p (r e) -> p r e", e=E)
            landed(nc.vector.reduce_max(row_max[:], raw_logits, AX_X))
            row_all = row_max[:].rearrange("p (r a) -> p r a", a=1).to_broadcast(tiles_e)
            nc.vector.tensor_sub(logits, raw_logits, row_all).then_inc(shifted, 1)
            dve.wait_ge(exp_done, 1)
            landed(nc.vector.reduce_sum(row_max[:], probs, AX_X))
            landed(nc.vector.reciprocal(row_max[:], row_max[:]))
            landed(nc.vector.tensor_mul(probs, probs, row_all))
            for r in range(TILES):
                largest = nc.vector.max(top_p[:, r, :], probs[:, r, :])
            landed(largest)
            for r in range(TILES):
                where = nc.vector.max_index(top_i[:, r, :], top_p[:, r, :], probs[:, r, :])
            tiles_k = [P, TILES, TOP_E]
            nc.vector.tensor_sub(mix[:], top_p[:, :, 0:TOP_E], top_p[:, :, 0:1].to_broadcast(tiles_k)
                                 ).then_inc(mix_shifted, 1)
            landed(where)
            hot_shape = [P, TOP_E, TILES, E]
            landed(nc.vector.tensor_tensor(
                hot, expert_no[:].rearrange("p (a b e) -> p a b e", a=1, b=1).to_broadcast(hot_shape),
                top_i[:, :, 0:TOP_E].rearrange("p r (k a) -> p k r a", a=1).to_broadcast(hot_shape), ALU.is_equal))
            with nc.allow_low_precision("sums of at most three zeros and ones"):
                nc.vector.tensor_reduce(chosen[:], hot.rearrange("p k r e -> p r e k"), AX_X, ALU.add
                                        ).then_inc(chosen_done, 1)
            dve.wait_ge(counts_done, 1)
            landed(nc.vector.tensor_tensor(
                over, count_ps.rearrange("p (e a) -> p e a", a=1).to_broadcast([P, E, TILES]),
                tile_start[:].rearrange("p (a r) -> p a r", a=1).to_broadcast([P, E, TILES]), ALU.is_gt))
            landed(nc.vector.reduce_sum(slots_of[:], over, AX_X))
            landed(nc.vector.tensor_mul(before_e, earlier[:], slots_of[:].rearrange("p (a e) -> p a e", a=1)
                                        .to_broadcast([P, E, E])))
            landed(nc.vector.reduce_sum(first_slot[:], before_e, AX_X))
            dve.wait_ge(counts_done, 2)
            landed(nc.vector.scalar_tensor_tensor(
                out=place, in0=first_slot[:].rearrange("p (a e) -> p a e", a=1).to_broadcast(tiles_e),
                scalar=float(P), in1=rank_ps.rearrange("p (r e) -> p r e", e=E), op0=ALU.mult, op1=ALU.add))
            landed(nc.vector.tensor_mul(
                hot_x, hot, place.rearrange("p (a r) e -> p a r e", a=1).to_broadcast(hot_shape)))
            with nc.allow_low_precision("whole numbers below 2^13"):
                landed(nc.vector.reduce_sum(pos_i[:, 0, :], hot_x.rearrange("p k r e -> p (k r) e"), AX_X))
            nc.vector.tensor_single_scalar(pos_i[:, 1, :], pos_i[:, 0, :], 7, ALU.arith_shift_right)
            landed(nc.vector.tensor_single_scalar(pos_i[:, 2, :], pos_i[:, 0, :], P - 1, ALU.bitwise_and))
            landed(nc.vector.tensor_copy(pos_h[:], pos_i[:, 1:3, :]))
            pair_slots, pair_rows = [P, SLOTS, PAIRS], [P, P, PAIRS]
            nc.vector.tensor_tensor(
                slot_hot[:], slot_no_h[:], pos_h[:, 0, :].rearrange("p (a m) -> p a m", a=1).to_broadcast(pair_slots),
                ALU.is_equal).then_inc(places_known, 1)
            nc.vector.tensor_tensor(
                row_hot, row_no[:], pos_h[:, 1, :].rearrange("p (a m) -> p a m", a=1).to_broadcast(pair_rows),
                ALU.is_equal)
            dve.wait_ge(places_known, 1)
            nc.vector.tensor_mul(
                slot_token[:], slot_hot[:],
                token_1[:].rearrange("p (a k) r -> p a (k r)", a=1).to_broadcast(pair_slots)).then_inc(places_done, 1)
            landed(nc.vector.tensor_add(end_slot[:], first_slot[:], slots_of[:]))
            dve.wait_ge(tokens_done, 1)
            nc.vector.tensor_scalar(gather_idx[:], token_ps, -1.0, 0.0, ALU.add, ALU.max).then_inc(indices_done, 1)
            landed(nc.vector.tensor_scalar(empty[:], token_ps, 0.0, spare_1[:], ALU.is_equal, ALU.mult))
            nc.vector.scalar_tensor_tensor(out=scatter_idx[:], in0=token_ps, scalar=-1.0, in1=empty[:],
                                           op0=ALU.add, op1=ALU.add).then_inc(indices_done, 1)
            slot_e = [P, SLOTS, E]
            landed(nc.vector.tensor_tensor(
                passed, slot_no[:].rearrange("p (s a) -> p s a", a=1).to_broadcast(slot_e),
                end_slot[:].rearrange("p (a e) -> p a e", a=1).to_broadcast(slot_e), ALU.is_ge))
            landed(nc.vector.reduce_sum(slot_expert_f[:], passed, AX_X))
            nc.vector.tensor_scalar(slot_expert[:], slot_expert_f[:], float(E - 1), None, ALU.min).then_inc(
                experts_known, 1)

            def expert_of(s):
                return dve.value_load(slot_expert[0:1, bass.ds(s, 1)], min_val=0, max_val=E - 1)

            w1_flat = w1_sb[:].rearrange("p e k i -> p (e k i)")

            def copy_w1(s, odd, e):
                if not isinstance(s, int) or s >= 2:
                    dve.wait_ge(hidden_done, s - 1)
                nc.vector.tensor_copy(slot_w1[:, odd, :], w1_flat[:, bass.ds(e * (KT * HID), KT * HID)]
                                      ).then_inc(w1_ready, 1)

            dve.wait_ge(experts_known, 1)
            dve.wait_ge(weights_loaded, 32 * E)
            copy_w1(0, 0, expert_of(0))
            copy_w1(1, 1, expert_of(1))
            dve.wait_ge(mix_exp_done, 1)
            landed(nc.vector.reduce_sum(row_max[:], mix[:], AX_X))
            landed(nc.vector.reciprocal(row_max[:], row_max[:]))
            landed(nc.vector.tensor_mul(mix[:], mix[:], row_max[:].rearrange("p (r a) -> p r a", a=1)
                                        .to_broadcast(tiles_k)))
            landed(nc.vector.tensor_mul(
                hot_x, hot, mix[:].rearrange("p r (k a) -> p k r a", a=1).to_broadcast(hot_shape)))
            nc.vector.tensor_reduce(row_weight[:], hot_x.rearrange("p k r e -> p e (k r)"), AX_X, ALU.add
                                    ).then_inc(chosen_done, 1)
            landed(nc.vector.tensor_scalar(count[:], count_ps, 1.0, None, ALU.max))
            landed(nc.vector.reciprocal(count[:], count[:]))
            dve.wait_ge(counts_done, 3)
            nc.vector.tensor_mul(weight[:], mix_ps, count[:]).then_inc(y_biased, 1)
            dve.wait_ge(y_biased, 1)

            def finish_slot(s, odd, e):
                dve.wait_ge(y_done, s + 1)
                if not isinstance(s, int) or s >= 2:
                    dve.wait_ge(sum_landed, s * 16 - 16)
                nc.vector.tensor_add(y_sb[:, odd, :], y_ps[odd], b2_bc[:, bass.ds(e * D, D)]).then_inc(y_biased, 1)
                dve.wait_ge(y_biased, s + 2)
                nc.vector.tensor_scalar(y_sb[:, odd, :], y_sb[:, odd, :], weight[:, bass.ds(e, 1)], None, ALU.mult
                                        ).then_inc(y_ready, 1)

            copy_w1(2, 0, expert_of(2))
            finish_slot(0, 0, expert_of(0))
            copy_w1(3, 1, expert_of(3))
            finish_slot(1, 1, expert_of(1))
            with dve.Fori(1, (SLOTS - 3) // 2) as i:
                copy_w1(i * 2 + 2, 0, expert_of(i * 2 + 2))
                finish_slot(i * 2, 0, expert_of(i * 2))
                copy_w1(i * 2 + 3, 1, expert_of(i * 2 + 3))
                finish_slot(i * 2 + 1, 1, expert_of(i * 2 + 1))
            copy_w1(SLOTS - 1, 0, expert_of(SLOTS - 1))
            for s in range(SLOTS - 3, SLOTS):
                finish_slot(s, s % 2, expert_of(s))

            for b in range(B):
                dve.wait_ge(total_loaded[b], 16)
                nc.vector.tensor_add(both_halves[:, b, :], total_sb[:, b * HALVES, :], total_sb[:, b * HALVES + 1, :]
                                     ).then_inc(halves_added, 1)
            dve.wait_ge(pooled_done, 1)
            nc.vector.tensor_copy(pooledT[:], pool_ps).then_inc(pooled_copied, 1)
            dve.wait_ge(phi_copied, 1)
            nc.vector.tensor_scalar(factor[:], phi[:], 0.7, -0.8, ALU.is_gt, ALU.mult).then_inc(end_step, 1)
            dve.wait_ge(end_step, 1)
            nc.vector.tensor_scalar(factor[:], factor[:], 1.0, gate[:, 1:2], ALU.add, ALU.mult).then_inc(end_step, 1)
            dve.wait_ge(end_step, 2)
            for b in range(B):
                rows = x1_sb[:, b * HALVES:(b + 1) * HALVES, :]
                nc.vector.scalar_tensor_tensor(
                    out=rows, in0=total_sb[:, b * HALVES:(b + 1) * HALVES, :], scalar=factor[:, b:b + 1],
                    in1=rows, op0=ALU.mult, op1=ALU.add).then_inc(out_ready, 1)


_INS = ["x", "ctx_512", "g_xattn", "g_ffn", "L0_xattn_Wq", "L0_xattn_Wk", "L0_xattn_gamma_raw", "L0_ffn_Wr",
        "L0_ffn_br", "L0_ffn_w1", "L0_ffn_b1", "L0_ffn_w2", "L0_ffn_b2", "L0_ffn_Wp1", "L0_ffn_bp1",
        "L0_ffn_Wp2", "L0_ffn_bp2"]


def kernel(**inputs):
    import numpy as _np
    import concourse.bacc as _bacc
    from concourse import mybir as _mybir
    from concourse.bass_utils import run_bass_kernel_spmd as _run

    nc = _bacc.Bacc("TRN2", target_bir_lowering=False, num_devices=1, dynamic_dma_scratch_size=8192)
    arrays, args = {}, []
    for name in _INS:
        a = _np.ascontiguousarray(inputs[name])
        arrays[f"in_{name}_dram"] = a
        args.append(nc.dram_tensor(f"in_{name}_dram", a.shape, _mybir.dt.from_np(a.dtype), kind="ExternalInput").ap())
    out = nc.dram_tensor("out_0_dram", (B, S, D), _mybir.dt.float32, kind="ExternalOutput").ap()
    flamingo_block(nc, *args, out)
    r = _run(nc, [arrays], core_ids=[0])
    return r.results[0]["out_0_dram"]
```
